# Optimizing a Trainium2 kernel written in Bass

```python
import numpy as np
import jax
import jax.numpy as jnp

def _softmax(x, axis=-1):
    return jax.nn.softmax(x, axis=axis)

def _gelu(x):
    return jax.nn.gelu(x, approximate=True)

def _silu(x):
    return jax.nn.silu(x)

def _sigmoid(x):
    return jax.nn.sigmoid(x)

def _layernorm(x, axis=-1, eps=1e-05):
    m = jnp.mean(x, axis=axis, keepdims=True)
    v = jnp.var(x, axis=axis, keepdims=True)
    return (x - m) / jnp.sqrt(v + eps)

def _scatter_add(tgt, idx, src, axis=0):
    return tgt.at[idx].add(src)

def _segment_sum(src, seg, n):
    return jax.ops.segment_sum(src, seg, n)
kernel_name = 'mk_gnn_resnorm_d2_gnn_r8_dfe0d1'

def setup_inputs(seed: int=0):
    np.random.seed(seed)
    _w = jnp.asarray

    def _rec_inputs():
        import jax
        import jax.numpy as jnp
        _gk = jax.random.key(seed)
        x = -0.000202 + 1 * jax.random.normal(jax.random.fold_in(_gk, 1), (12500, 64), jnp.float32)
        src = jax.random.randint(jax.random.fold_in(_gk, 2), (400000,), 0, 12500, jnp.int32)
        dst = jax.random.randint(jax.random.fold_in(_gk, 3), (400000,), 0, 12500, jnp.int32)
        _o = jnp.argsort(dst, stable=True)
        src = src[_o]
        dst = dst[_o]
        edge_attr_32 = -5.16925e-05 + 1.00005 * jax.random.normal(jax.random.fold_in(_gk, 12), (400000, 32), jnp.float32)
        return (x, src, dst, edge_attr_32)
    x, src, dst, edge_attr_32 = _rec_inputs()

    def _L0_gnn_setup():
        import jax, jax.numpy as jnp
        import numpy as np
        N_NODES = 12500
        N_EDGES = 400000
        EDGE_OUT = 32
        HID = 128
        NODE_OUT = 64
        N_GRAPHS = 16
        key = jax.random.key(seed)
        ks = jax.random.split(key, 9)
        x = jax.random.normal(ks[0], (N_NODES, 64), dtype=jnp.float32)
        edge_index = jax.random.randint(ks[1], (2, N_EDGES), 0, N_NODES, dtype=jnp.int64)
        edge_attr = jax.random.normal(ks[2], (N_EDGES, EDGE_OUT), dtype=jnp.float32)
        u = jax.random.normal(ks[3], (N_GRAPHS, 1), dtype=jnp.float32)
        batch = jnp.sort(jax.random.randint(ks[4], (N_NODES,), 0, N_GRAPHS, dtype=jnp.int64))
        d_in = 3 * EDGE_OUT + 1
        W1 = jax.random.normal(ks[5], (d_in, HID), dtype=jnp.float32) / np.sqrt(d_in)
        b1 = jnp.zeros((HID,), dtype=jnp.float32)
        W2 = jax.random.normal(ks[6], (HID, NODE_OUT), dtype=jnp.float32) / np.sqrt(HID)
        b2 = jnp.zeros((NODE_OUT,), dtype=jnp.float32)
        return {'x': x, 'edge_index': edge_index, 'edge_attr': edge_attr, 'u': u, 'batch': batch, 'W1': W1, 'b1': b1, 'W2': W2, 'b2': b2}
    _L0_gnn_all = _L0_gnn_setup()
    _L0_gnn_in = {k: v for k, v in _L0_gnn_all.items() if k in ('u', 'W1', 'b1', 'W2', 'b2')}
    del _L0_gnn_all

    def _L1_gnn_setup():
        import jax, jax.numpy as jnp
        import numpy as np
        N_NODES = 12500

        def _gcn_layer(x, W, b, src, dst, n):
            h = x @ W
            loops = jnp.arange(n, dtype=src.dtype)
            s = jnp.concatenate([src, loops])
            d = jnp.concatenate([dst, loops])
            deg = jax.ops.segment_sum(jnp.ones_like(d, dtype=h.dtype), d, num_segments=n)
            dis = jnp.where(deg > 0, jax.lax.rsqrt(jnp.maximum(deg, 1.0)), 0.0)
            norm = dis[s] * dis[d]
            msg = h[s] * norm[:, None]
            out = jax.ops.segment_sum(msg, d, num_segments=n)
            return out + b
        key = jax.random.key(seed)
        k1, k2, k3, k4, k5 = jax.random.split(key, 5)
        in_feat, hidden, out_feat = (64, 128, 64)
        n_edges = 200000
        node_features = jax.random.normal(k1, (N_NODES, in_feat), dtype=jnp.float32)
        edge_index = jax.random.randint(k2, (2, n_edges), 0, N_NODES, dtype=jnp.int32)
        W1 = jax.random.normal(k3, (in_feat, hidden), dtype=jnp.float32) * (1.0 / np.sqrt(in_feat))
        b1 = jnp.zeros((hidden,), dtype=jnp.float32)
        W2 = jax.random.normal(k4, (hidden, out_feat), dtype=jnp.float32) * (1.0 / np.sqrt(hidden))
        b2 = jnp.zeros((out_feat,), dtype=jnp.float32)
        return {'node_features': node_features, 'edge_index': edge_index, 'W1': W1, 'b1': b1, 'W2': W2, 'b2': b2}
    _L1_gnn_all = _L1_gnn_setup()
    _L1_gnn_in = {k: v for k, v in _L1_gnn_all.items() if k in ('W1', 'b1', 'W2', 'b2')}
    del _L1_gnn_all
    return {'x': x, 'src': src, 'dst': dst, 'edge_attr_32': edge_attr_32, 'L0_gnn_u': _L0_gnn_in['u'], 'L0_gnn_W1': _L0_gnn_in['W1'], 'L0_gnn_b1': _L0_gnn_in['b1'], 'L0_gnn_W2': _L0_gnn_in['W2'], 'L0_gnn_b2': _L0_gnn_in['b2'], 'L1_gnn_W1': _L1_gnn_in['W1'], 'L1_gnn_b1': _L1_gnn_in['b1'], 'L1_gnn_W2': _L1_gnn_in['W2'], 'L1_gnn_b2': _L1_gnn_in['b2']}

def reference(x, src, dst, edge_attr_32, L0_gnn_u, L0_gnn_W1, L0_gnn_b1, L0_gnn_W2, L0_gnn_b2, L1_gnn_W1, L1_gnn_b1, L1_gnn_W2, L1_gnn_b2):
    import jax
    import jax.numpy as jnp

    def _L0_gnn_ref(x, edge_index, edge_attr, u, batch, W1, b1, W2, b2):
        import jax, jax.numpy as jnp
        import numpy as np
        N_NODES = 12500
        N_EDGES = 400000
        EDGE_OUT = 32
        HID = 128
        NODE_OUT = 64
        N_GRAPHS = 16
        N = x.shape[0]
        row = edge_index[0]
        seg_sum = jax.ops.segment_sum(edge_attr, row, num_segments=N)
        seg_max = jax.ops.segment_max(edge_attr, row, num_segments=N)
        cnt = jax.ops.segment_sum(jnp.ones((edge_attr.shape[0], 1), edge_attr.dtype), row, num_segments=N)
        seg_mean = seg_sum / jnp.maximum(cnt, 1.0)
        seg_max = jnp.where(cnt > 0, seg_max, 0.0)
        h = jnp.concatenate([seg_sum, seg_max, seg_mean, u[batch]], axis=1)
        h = jax.nn.relu(h @ W1 + b1)
        return h @ W2 + b2

    def _L1_gnn_ref(node_features, edge_index, W1, b1, W2, b2):
        import jax, jax.numpy as jnp
        import numpy as np
        N_NODES = 12500

        def _gcn_layer(x, W, b, src, dst, n):
            h = x @ W
            loops = jnp.arange(n, dtype=src.dtype)
            s = jnp.concatenate([src, loops])
            d = jnp.concatenate([dst, loops])
            deg = jax.ops.segment_sum(jnp.ones_like(d, dtype=h.dtype), d, num_segments=n)
            dis = jnp.where(deg > 0, jax.lax.rsqrt(jnp.maximum(deg, 1.0)), 0.0)
            norm = dis[s] * dis[d]
            msg = h[s] * norm[:, None]
            out = jax.ops.segment_sum(msg, d, num_segments=n)
            return out + b
        src, dst = (edge_index[0], edge_index[1])
        n = node_features.shape[0]
        h = _gcn_layer(node_features, W1, b1, src, dst, n)
        h = jax.nn.relu(h)
        h = _gcn_layer(h, W2, b2, src, dst, n)
        return h
    edge_index = jnp.stack([src, dst])
    batch0 = jnp.zeros((12500,), jnp.int32)
    x = _layernorm(x + _L0_gnn_ref(x, edge_index, edge_attr_32, L0_gnn_u, batch0, L0_gnn_W1, L0_gnn_b1, L0_gnn_W2, L0_gnn_b2), axis=-1)
    x = _layernorm(x + _L1_gnn_ref(x, edge_index, L1_gnn_W1, L1_gnn_b1, L1_gnn_W2, L1_gnn_b2), axis=-1)
    return x

_drawn_inputs = setup_inputs


def setup_inputs(seed=0):
    import zlib

    import numpy as np

    out = dict(_drawn_inputs(seed))
    spreads = {'L0_gnn_b1': (0.0, 0.1),
     'L0_gnn_b2': (0.0, 0.1),
     'L1_gnn_b1': (0.0, 0.1),
     'L1_gnn_b2': (0.0, 0.1)}
    factors = {'L0_gnn_u': 2.777}
    for name, (base, spread) in spreads.items():
        noise = np.random.default_rng([zlib.crc32(name.encode()), seed]).standard_normal(out[name].shape)
        drawn = base * np.exp(spread * noise) if base else spread * noise
        out[name] = jnp.asarray(drawn.astype(out[name].dtype))
    for name, factor in factors.items():
        out[name] = (out[name] * factor).astype(out[name].dtype)
    return out
```

```python
from contextlib import ExitStack

import concourse.bass as bass
from concourse import mybir

F32, BF16, I32 = mybir.dt.float32, mybir.dt.bfloat16, mybir.dt.int32
ALU = mybir.AluOpType
ACT = mybir.ActivationFunctionType
AX = mybir.AxisListType.X

P = 128
N, E = 12500, 400000
COLS = E // P
W = -(-N // P)
NPAD = W * P
LASTROWS = N - (W - 1) * P
D, A, HID = 64, 32, 128
ROW = A + 1
GT = 5
GROUPS = COLS // GT
SJ = 125
SCHUNKS = COLS // SJ
CJ = 25
CHUNKS = COLS // CJ
SW = 7
STEPS = W // SW
BIG = 3.4e38
EPS = 1e-5
assert E % P == 0 and GROUPS * GT == COLS and GROUPS % 2 and SCHUNKS % 2 and CHUNKS % 2 and STEPS * SW == W


def paired(eng, count, body):
    pairs = count // 2
    body(0, 0, 0)
    body(1, 1, 0)
    with eng.Fori(1, pairs) as i:
        body(i * 2, 0, i)
        body(i * 2 + 1, 1, i)
    if count % 2:
        body(count - 1, 0, pairs)


def build(nc, x, src, dst, attr, u, w1, b1, w2, b2, v1, c1, v2, c2, out):
    with ExitStack() as ctx:
        def sb(name, shape, dt=F32):
            return ctx.enter_context(nc.sbuf_tensor(name, shape, dt))

        def pair(name, shape, dt=F32):
            return [sb(f"{name}{h}", shape, dt) for h in range(2)]

        def sem(name):
            return ctx.enter_context(nc.semaphore(name))

        def dram(name, shape):
            return nc.dram_tensor(name, shape, F32, kind="Internal").ap()

        by_src = dram("by_src", (E + 2, ROW))
        running = [dram(f"running{k}", (E + 1, D)) for k in range(3)]
        correction = [dram(f"correction{k}", (NPAD, D)) for k in range(3)]
        table = [dram(f"table{k}", (NPAD, D)) for k in range(2)]

        def node_view(t):
            return t.rearrange("(w l) f -> l w f", l=P)

        def edge_view(t, first=0):
            return t[first:first + E, :].rearrange("(p j) f -> p (j f)", p=P)

        ps = ctx.enter_context(nc.psum_tensor("ps", [P, 8 * 512], F32))
        ps_src = ps[:, 0:W]
        ps_dst = ps[:, 512:512 + W]
        ps_small = [ps[:, 1024:1024 + W], ps[:, 1024 + P:1024 + P + W]]
        ps_lot = ps[:, 1024:1024 + GT * P // 2].bitcast(BF16)
        ps_same = ps[:, 1536:1536 + GT * P]
        ps_rank = [ps[:, 2560 + 512 * h:2560 + 512 * h + GT * W] for h in range(2)]
        HALF = SW * P // 2
        ps_cat = ps[:, 1536:1536 + SW * P]
        ps_hid = [ps[:, 2560 + 512 * h:2560 + 512 * h + HALF] for h in range(2)]
        ps_node = ps[:, 3584:3584 + SW * D]
        ps_turn = ps[:, 0:512]

        diff = sb("diff", [P, P], I32)
        col_i = sb("col_i", [P, P], I32)
        col = sb("col", [P, P], BF16)
        ident = sb("ident", [P, P])
        ident_b = sb("ident_b", [P, P], BF16)
        before = sb("before", [P, P])
        before_b = sb("before_b", [P, P], BF16)
        ones = sb("ones", [P, P])
        zeros_b = sb("zeros_b", [P, P], BF16)
        nothing = pair("nothing", [P, SW, D])
        sentinel = sb("sentinel", [P, D])

        arena = sb("arena", [P, 2 * SJ * D])
        scan_out = [arena[:, h * SJ * D:(h + 1) * SJ * D].rearrange("p (j f) -> p j f", f=D) for h in range(2)]
        agg = arena[:, 0:W * D].rearrange("p (w f) -> p w f", f=D)
        ys = arena[:, SJ * D:SJ * D + W * D].rearrange("p (w f) -> p w f", f=D)
        dst_i = arena[:, 0:COLS].bitcast(I32)
        part = [arena[:, (k + 1) * COLS:(k + 2) * COLS].bitcast(I32) for k in range(4)]
        INLEN = (SJ + 1) * ROW
        arena2 = sb("arena2", [P, 2 * INLEN])
        keys = arena2[:, 0:2 * COLS].bitcast(BF16).rearrange("p (j k) -> p j k", k=4)
        scan_in = [arena2[:, h * INLEN:(h + 1) * INLEN] for h in range(2)]
        got_rows = [arena2[:, h * CJ * D:(h + 1) * CJ * D].rearrange("p (j f) -> p j f", f=D) for h in range(2)]

        src_i = sb("src_i", [P, COLS], I32)
        cont = sb("cont", [P, COLS])

        stage = pair("stage", [P, GT, 4], BF16)
        stage_f = pair("stage_f", [P, GT, 4])
        lo = pair("lo", [P, GT, P], BF16)
        hi = pair("hi", [P, GT, W], BF16)
        dlo = pair("dlo", [P, GT, P], BF16)
        dhi = pair("dhi", [P, GT, W], BF16)
        lot_b = sb("lot_b", [P, GT * P], BF16)
        lot_f = sb("lot_f", [P, GT * P])
        same = sb("same", [P, GT, P], BF16)
        snap = pair("snap", [P, W])
        picked = sb("picked", [P, GT, W])
        rank = pair("rank", [P, GT], I32)
        attr_in = pair("attr_in", [P, GT, A])
        rows = pair("rows", [P, GT, ROW])

        flag = sb("flag", [P, SJ])
        sign = sb("sign", [P, SJ])
        limit = sb("limit", [P, SJ])
        whole_c = sb("whole_c", [P, SCHUNKS])
        gflag = pair("gflag", [P, CJ])
        gidx = pair("gidx", [P, CJ], I32)

        cnt = pair("cnt", [P, W])
        total = sb("total", [P, W])
        incl = sb("incl", [P, W])
        base = sb("base", [P, W])
        has = sb("has", [P, W])
        last = sb("last", [P, W])
        end_row = pair("end_row", [P, W], I32)
        inv_cnt = sb("inv_cnt", [P, W])
        root = sb("root", [P, W])
        dis = sb("dis", [P, W])
        xs = sb("xs", [P, W, D])
        corr = pair("corr", [P, SW, D])
        cat = pair("cat", [P, SW, 3 * A])
        cat_t = sb("cat_t", [3 * A, SW * P])
        hid = sb("hid", [P, SW * P])
        mid = sb("mid", [P, SW, D])
        sq = sb("sq", [P, SW, D])
        res = pair("res", [P, SW, D])
        stat = sb("stat", [P, 4, SW])

        whole = pair("whole", [P, 1])
        edge_key = [sb(f"edge_key{k}", [P, 3]) for k in range(2)]
        first_cont = pair("first_cont", [P, 1])
        dst_side = sb("dst_side", [P, 2], I32)
        work = sb("work", [P, 4])
        target = pair("target", [P, 1], I32)
        whole_w = sb("whole_w", [P, D])
        turned = sb("turned", [D, 2 * P])
        sign_t = sb("sign_t", [D, P])
        limit_t = sb("limit_t", [D, P])
        carry_t = sb("carry_t", [D, P + 1])
        carry = sb("carry", [P, D])

        w1_s = sb("w1_s", [3 * A, HID])
        w2_s = sb("w2_s", [HID, D])
        v1_s = sb("v1_s", [D, HID])
        v2_s = sb("v2_s", [HID, D])
        bcol = sb("bcol", [P, 4])
        bias0 = sb("bias0", [P, 1])
        b2_s = sb("b2_s", [P, D])
        c2_s = sb("c2_s", [P, D])

        s_src, s_dst, s_x, s_w, s_iota, s_const, s_init, s_keep = (sem(n) for n in (
            "s_src", "s_dst", "s_x", "s_w", "s_iota", "s_const", "s_init", "s_keep"))
        s_part, s_keys, s_xready, s_xpad = (sem(n) for n in ("s_part", "s_keys", "s_xready", "s_xpad"))
        a_zeroed, a_staged, a_onehot, a_used = (sem(n) for n in ("a_zeroed", "a_staged", "a_onehot", "a_used"))
        n_cnt, n_sums, n_chain, n_seed, n_deg, n_root = (sem(n) for n in (
            "n_cnt", "n_sums", "n_chain", "n_seed", "n_deg", "n_root"))
        b_staged, b_onehot, b_used, b_turned, b_copied, b_same, b_masked = (sem(n) for n in (
            "b_staged", "b_onehot", "b_used", "b_turned", "b_copied", "b_same", "b_masked"))
        b_snap, b_state, b_ranked, b_picked, b_pos, b_rows, b_seen = (sem(n) for n in (
            "b_snap", "b_state", "b_ranked", "b_picked", "b_pos", "b_rows", "b_seen"))
        b_attr = [sem(f"b_attr{h}") for h in range(2)]
        b_scat = [[sem(f"b_scat{h}_{k}") for k in range(GT)] for h in range(2)]
        c_in = [sem(f"c_in{h}") for h in range(2)]
        c_out = [sem(f"c_out{h}") for h in range(2)]
        c_next, c_flag, c_scan = sem("c_next"), sem("c_flag"), sem("c_scan")
        g_staged, g_seen, g_flag, g_chain = (sem(n) for n in (
            "g_staged", "g_seen", "g_flag", "g_chain"))
        g_got = [[sem(f"g_got{h}_{k}") for k in range(CJ)] for h in range(2)]
        g_out = [sem(f"g_out{h}") for h in range(2)]
        k_chain, k_turned, k_back, k_scat = (sem(n) for n in (
            "k_chain", "k_turned", "k_back", "k_scat"))
        m_got = [[sem(f"m_got{h}_{k}") for k in range(SW)] for h in range(2)]
        m_corr = [sem(f"m_corr{h}") for h in range(2)]
        m_link, m_cat, m_turned, m_copied, m_hid, m_relu, m_node, m_chain, m_var, m_root, m_done = (
            sem(n) for n in ("m_link", "m_cat", "m_turned", "m_copied", "m_hid", "m_relu", "m_node",
                             "m_chain", "m_var", "m_root", "m_done"))
        m_store = [sem(f"m_store{h}") for h in range(2)]
        ctx.enter_context(nc.allow_non_contiguous_dma(reason="columns of 128 numbers"))
        ctx.enter_context(nc.allow_low_precision(reason="a sum with one term that isn't zero, a whole number"))
        block = ctx.enter_context(nc.Block())

        SRC_GROUPS = [313, 312]
        G_HALF = [CHUNKS - CHUNKS // 2, CHUNKS // 2]
        C_HALF = [SCHUNKS - SCHUNKS // 2, SCHUNKS // 2]
        LINKS = COLS - 1
        assert SRC_GROUPS[0] == GROUPS - GROUPS // 2
        INIT = 16 * (3 * STEPS + 3 + 2)
        WLOAD = 16 * 10

        def at_end(g, count):
            return isinstance(g, int) and g == count - 1

        def at_start(g):
            return isinstance(g, int) and g < 2

        @block.sync
        def _(sp):
            sp.dma_start(src_i[:, :], src.rearrange("(p j) -> p j", p=P)).then_inc(s_src, 16)
            sp.dma_start(dst_i, dst.rearrange("(p j) -> p j", p=P)).then_inc(s_dst, 16)
            sp.wait_ge(s_xpad, 1)
            dst_rows = dst.rearrange("(p j a) -> p j a", p=P, a=1)
            sp.dma_start(dst_side[1:P, 0:1], dst_rows[0:P - 1, COLS - 1, :]).then_inc(s_dst, 16)
            sp.dma_start(dst_side[0:P - 1, 1:2], dst_rows[1:P, 0, :]).then_inc(s_dst, 16)
            sp.dma_start(xs[:, 0:W - 1, :],
                         x[0:(W - 1) * P, :].rearrange("(w l) f -> l w f", l=P)).then_inc(s_x, 16)
            sp.dma_start(xs[0:LASTROWS, W - 1, :], x[(W - 1) * P:N, :]).then_inc(s_x, 16)
            for to, frm in ((w1_s[:, :], w1[0:3 * A, :]), (w2_s[:, :], w2), (v1_s[:, :], v1), (v2_s[:, :], v2),
                            (bcol[:, 0:1], b1.rearrange("(p a) -> p a", a=1)),
                            (bcol[:, 1:2], w1[3 * A:3 * A + 1, :].rearrange("a p -> p a")),
                            (bcol[:, 2:3], u[0:1, 0:1].to_broadcast([P, 1])),
                            (bcol[:, 3:4], c1.rearrange("(p a) -> p a", a=1)),
                            (b2_s[:, :], b2.rearrange("(a f) -> a f", a=1).to_broadcast([P, D])),
                            (c2_s[:, :], c2.rearrange("(a f) -> a f", a=1).to_broadcast([P, D]))):
                sp.dma_start(to, frm).then_inc(s_w, 16)
            sp.wait_ge(s_keep, 1)
            for k in range(3):
                sp.dma_start(running[k][E:E + 1, :], nothing[1][0:1, 0, :]).then_inc(s_init, 16)
            sp.dma_start(by_src[0:1, :], sentinel[0:1, 0:ROW]).then_inc(s_init, 16)
            sp.dma_start(by_src[E + 1:E + 2, :], sentinel[0:1, 0:ROW]).then_inc(s_init, 16)
            with sp.Fori(0, STEPS) as s:
                for k in range(3):
                    sp.dma_start(node_view(correction[k])[:, bass.ds(s * SW, SW), :],
                                 nothing[min(k, 1)][:, :, :]).then_inc(s_init, 16)

            def attributes(g, h, i):
                if not at_start(g):
                    sp.wait_ge(b_rows, g - 1)
                sp.dma_start(attr_in[h].rearrange("p t a -> p (t a)"),
                             edge_view(attr)[:, bass.ds(g * (GT * A), GT * A)]).then_inc(b_attr[h], 16)

            paired(sp, GROUPS, attributes)

            for h in range(2):
                for k in range(GT):
                    sp.wait_ge(b_scat[h][k], 16 * SRC_GROUPS[h])
            sp.wait_ge(s_init, INIT)
            sp.dma_start(edge_key[0][:, 2:3], by_src[2:E + 2, :].rearrange("(p j) f -> p j f", p=P)[
                :, COLS - 1, A:A + 1]).then_inc(c_next, 16)

            def scan_load(g, h, i):
                if not at_start(g):
                    sp.wait_ge(c_scan, g - 1)
                sp.dma_start(scan_in[h][:, 0:ROW],
                             edge_view(by_src)[:, bass.ds(g * (SJ * ROW), ROW)]).then_inc(c_in[h], 16)
                sp.dma_start(scan_in[h][:, ROW:INLEN],
                             edge_view(by_src, 1)[:, bass.ds(g * (SJ * ROW), SJ * ROW)]).then_inc(c_in[h], 16)

            paired(sp, SCHUNKS, scan_load)

            def step_load(mode):
                def load(g, h, i):
                    if mode or not at_start(g):
                        sp.wait_ge(m_cat, mode * STEPS + g - 1)
                    sp.dma_start(corr[h][:, :, :],
                                 node_view(correction[mode])[:, bass.ds(g * SW, SW), :]).then_inc(m_corr[h], 16)
                return load

            def step_store(mode):
                def store(g, h, i):
                    sp.wait_ge(m_done, mode * STEPS + g + 1)
                    if mode < 2:
                        sp.dma_start(node_view(table[mode])[:, bass.ds(g * SW, SW), :],
                                     ys[:, bass.ds(g * SW, SW), :]).then_inc(m_store[h], 16)
                    elif at_end(g, STEPS):
                        sp.dma_start(out[g * SW * P:(W - 1) * P, :].rearrange("(w l) f -> l w f", l=P),
                                     res[h][:, 0:SW - 1, :]).then_inc(m_store[h], 16)
                        sp.dma_start(out[(W - 1) * P:N, :], res[h][0:LASTROWS, SW - 1, :]).then_inc(m_store[h], 16)
                    else:
                        sp.dma_start(out[0:(W - 1) * P, :].rearrange("(w l) f -> l w f", l=P)[
                            :, bass.ds(g * SW, SW), :], res[h][:, :, :]).then_inc(m_store[h], 16)
                return store

            def node_io(mode):
                sp.wait_ge(k_scat, 16 * (mode + 1))
                load, store = step_load(mode), step_store(mode)
                load(0, 0, 0)

                def body(g, h, i):
                    load(g + 1, 1 - h, 0)
                    store(g, h, i)
                paired(sp, STEPS - 1, body)
                store(STEPS - 1, 1, 0)

            node_io(0)
            for q in range(2):
                def rows_out(g, h, i):
                    sp.wait_ge(g_chain, g * CJ + (q * LINKS + CJ - 1))
                    sp.dma_start(edge_view(running[q + 1])[:, bass.ds(g * (CJ * D), CJ * D)],
                                 got_rows[h].rearrange("p j f -> p (j f)")).then_inc(g_out[h], 16)
                paired(sp, CHUNKS, rows_out)
                node_io(q + 1)
            for h in range(2):
                sp.wait_ge(m_store[h], 16 * (3 * STEPS // 2 + h))

        @block.gpsimd
        def _(pool):
            nc.gpsimd.iota(diff[:, :], [[1, P]], base=0, channel_multiplier=-1).then_inc(s_iota, 1)
            nc.gpsimd.iota(col_i[:, :], [[1, P]], base=0, channel_multiplier=0).then_inc(s_iota, 1)

            def scatter(g, h, i):
                pool.wait_ge(b_pos, g + 1)
                pool.sem_inc(b_seen, 1)
                pool.wait_ge(b_rows, g + 1)
                pool.sem_inc(b_seen, 1)
                for k in range(GT):
                    nc.gpsimd.indirect_dma_start(
                        out=by_src, out_offset=bass.IndirectOffsetOnAxis(ap=rank[h][:, k:k + 1], axis=0),
                        in_=rows[h][:, k, :], in_offset=None).then_inc(b_scat[h][k], 16)

            pool.wait_ge(s_init, INIT)
            paired(pool, GROUPS, scatter)

            def aggregate(mode):
                pool.wait_ge(k_chain, 8 * mode + 8)
                nc.gpsimd.indirect_dma_start(
                    out=correction[mode],
                    out_offset=bass.IndirectOffsetOnAxis(ap=target[min(mode, 1)][:, 0:1], axis=0),
                    in_=carry[:, :], in_offset=None, bounds_check=NPAD - 1,
                    oob_is_err=False).then_inc(k_scat, 16)
                for h in range(2):
                    if mode == 0:
                        pool.wait_ge(c_out[h], 16 * C_HALF[h])
                    else:
                        pool.wait_ge(g_out[h], 16 * mode * G_HALF[h])
                if mode == 0:
                    pool.wait_ge(n_deg, 1)
                for w in range(W):
                    h, k, turn = w // SW % 2, w % SW, mode * STEPS // 2 + w // (2 * SW)
                    if turn:
                        pool.wait_ge(m_got[h][k], 16 * turn)
                    nc.gpsimd.indirect_dma_start(
                        out=agg[:, w, :], out_offset=None, in_=running[mode],
                        in_offset=bass.IndirectOffsetOnAxis(ap=end_row[min(mode, 1)][:, w:w + 1], axis=0),
                    ).then_inc(m_got[h][k], 16)

            aggregate(0)
            for q in range(2):
                for h in range(2):
                    pool.wait_ge(m_store[h], 16 * (q + 1) * (STEPS // 2))

                def gather(g, h, i):
                    pool.wait_ge(g_staged, g + (q * CHUNKS + 1))
                    pool.sem_inc(g_seen, 1)
                    if not at_start(g):
                        pool.wait_ge(g_out[h], i * 16 + 16 * q * G_HALF[h])
                        pool.sem_inc(g_seen, 1)
                        pool.wait_ge(g_chain, g * CJ + (q * LINKS - CJ))
                        pool.sem_inc(g_seen, 1)
                    for k in range(CJ):
                        nc.gpsimd.indirect_dma_start(
                            out=got_rows[h][:, k, :], out_offset=None, in_=table[q],
                            in_offset=bass.IndirectOffsetOnAxis(ap=gidx[h][:, k:k + 1], axis=0),
                            ).then_inc(g_got[h][k], 16)

                paired(pool, CHUNKS, gather)
                aggregate(q + 1)

        @block.scalar
        def _(act):
            def to_keys(k):
                act.wait_ge(s_part, k + 1)
                nc.scalar.copy(keys[:, :, k], part[k]).then_inc(s_keys, 1)

            to_keys(0)
            to_keys(1)
            to_keys(2)
            to_keys(3)

            def group(g, h, i):
                act.wait_ge(b_turned, g + 1)
                if not isinstance(g, int) or g > 0:
                    act.wait_ge(b_ranked, g)
                nc.scalar.copy(lot_b[:, :], ps_lot)
                nc.scalar.copy(lot_f[:, :], ps_lot).then_inc(b_copied, 1)
                act.wait_ge(b_attr[h], i * 16 + 16)
                if not at_start(g):
                    for k in range(GT):
                        act.wait_ge(b_scat[h][k], i * 16)
                nc.scalar.copy(rows[h][:, :, 0:A], attr_in[h][:, :, :])
                nc.scalar.copy(rows[h][:, :, A], src_i[:, bass.ds(g * GT, GT)]).then_inc(b_rows, 1)
                for t in range(GT):
                    act.wait_ge(b_state, g * GT + (t + 1))
                    nc.scalar.copy(snap[(t + h) % 2][:, :], ps_src).then_inc(b_snap, 1)

            paired(act, GROUPS, group)

            act.wait_ge(n_deg, 1)
            nc.scalar.activation(root[:, :], last[:, :], ACT.Sqrt).then_inc(n_root, 1)

            def scan_store(g, h, i):
                act.wait_ge(c_scan, g + 1)
                act.dma_start(edge_view(running[0])[:, bass.ds(g * (SJ * D), SJ * D)],
                              scan_out[h].rearrange("p j f -> p (j f)")).then_inc(c_out[h], 16)

            paired(act, SCHUNKS, scan_store)

            def node_step(mode):
                F = D if mode else 3 * A
                bias = bcol[:, 3:4] if mode else bias0[:, 0:1]

                def step(g, h, i):
                    if mode < 2:
                        act.wait_ge(m_turned, g + (mode * STEPS + 1))
                        nc.scalar.copy(cat_t[0:F, :], ps_cat[0:F, :]).then_inc(m_copied, 1)
                        act.wait_ge(m_hid, g + (mode * STEPS + 1))
                        for e in range(2):
                            last_one = nc.scalar.activation(hid[:, e * HALF:(e + 1) * HALF], ps_hid[e],
                                                            ACT.Relu, bias=bias)
                        last_one.then_inc(m_relu, 1)
                    if mode != 1:
                        act.wait_ge(m_var, g + (mode // 2 * STEPS + 1))
                        nc.scalar.activation(stat[:, 2, :], stat[:, 1, :], ACT.Sqrt).then_inc(m_root, 1)
                paired(act, STEPS, step)

            node_step(0)
            for q in range(2):
                def stage_idx(g, h, i):
                    if q or not at_start(g):
                        act.wait_ge(g_chain, g * CJ + (q * LINKS - CJ - 1))
                    nc.scalar.copy(gidx[h][:, :], src_i[:, bass.ds(g * CJ, CJ)]).then_inc(g_staged, 1)
                paired(act, CHUNKS, stage_idx)
                node_step(q + 1)

        @block.tensor
        def _(pe):
            pe.wait_ge(s_const, 1)
            nc.tensor.matmul(ps_src, zeros_b[:, :], zeros_b[:, 0:W], start=True, stop=False,
                             skip_group_check=True)
            nc.tensor.matmul(ps_dst, zeros_b[:, :], zeros_b[:, 0:W], start=True, stop=False,
                             skip_group_check=True)

            def count(g, h, i):
                pe.wait_ge(a_onehot, g + 1)
                for t in range(GT):
                    mm = nc.tensor.matmul(ps_src, lo[h][:, t, :], hi[h][:, t, :], start=False, stop=False,
                                          skip_group_check=True)
                mm.then_inc(a_used, 1)

            paired(pe, GROUPS, count)

            def prefix(k):
                pe.wait_ge(n_cnt, k + 1)
                nc.tensor.matmul(ps_small[0], before[:, :], cnt[k][:, :], start=True, stop=True)
                nc.tensor.matmul(ps_small[1], ones[:, :], cnt[k][:, :], start=True,
                                 stop=True).then_inc(n_sums, 1)

            prefix(0)
            pe.wait_ge(n_seed, 1)
            nc.tensor.matmul(ps_src, ident[:, :], base[:, :], start=True, stop=False,
                             skip_group_check=True).then_inc(b_state, 1)

            def group(g, h, i):
                pe.wait_ge(b_onehot, g + 1)
                if not isinstance(g, int) or g > 0:
                    pe.wait_ge(b_copied, g)
                for t in range(GT):
                    mm = nc.tensor.transpose(ps_lot[:, t * P:(t + 1) * P], lo[h][:, t, :], ident_b[:, :])
                mm.then_inc(b_turned, 1)
                for t in range(GT):
                    nc.tensor.matmul(ps_dst, dlo[h][:, t, :], dhi[h][:, t, :], start=False, stop=False,
                                     skip_group_check=True)
                pe.wait_ge(b_copied, g + 1)
                for t in range(GT):
                    one = lot_b[:, t * P:(t + 1) * P]
                    mm = nc.tensor.matmul(ps_same[:, t * P:(t + 1) * P], one, one, start=True, stop=True)
                mm.then_inc(b_same, 1)
                for t in range(GT):
                    pe.wait_ge(b_snap, g * GT + (t + 1))
                    nc.tensor.matmul(ps_rank[h][:, t * W:(t + 1) * W], lot_f[:, t * P:(t + 1) * P],
                                     snap[(t + h) % 2][:, :], start=(t == 0), stop=False,
                                     skip_group_check=True)
                    nc.tensor.matmul(ps_src, lo[h][:, t, :], hi[h][:, t, :], start=False, stop=False,
                                     skip_group_check=True).then_inc(b_state, 1)
                pe.wait_ge(b_masked, g + 1)
                for t in range(GT):
                    mm = nc.tensor.matmul(ps_rank[h][:, t * W:(t + 1) * W], same[:, t, :], hi[h][:, t, :],
                                          start=False, stop=(t == GT - 1), skip_group_check=True)
                mm.then_inc(b_ranked, 1)

            paired(pe, GROUPS, group)
            prefix(1)

            def turn(mode):
                pe.wait_ge(k_chain, 8 * mode + 2)
                tail = scan_out[0][:, SJ - 1, :] if mode == 0 else got_rows[0][:, CJ - 1, :]
                nc.tensor.transpose(ps_turn[0:D, 0:P], whole_w[:, :], ident[:, :])
                nc.tensor.transpose(ps_turn[0:D, P:2 * P], tail, ident[:, :]).then_inc(k_turned, 1)
                pe.wait_ge(k_chain, 8 * mode + 7)
                nc.tensor.transpose(ps_turn[:, 2 * P:2 * P + D], carry_t[:, 0:P], ident[0:D, 0:D]
                                    ).then_inc(k_back, 1)

            def node_step(mode):
                F, wa, wb = (D, v1_s, v2_s) if mode else (3 * A, w1_s, w2_s)

                def step(g, h, i):
                    k = g + (mode * STEPS + 1)
                    pe.wait_ge(m_cat, k)
                    for t in range(SW):
                        mm = nc.tensor.transpose(ps_cat[0:3 * A, t * P:(t + 1) * P], cat[h][:, t, :], ident[:, :])
                    mm.then_inc(m_turned, 1)
                    pe.wait_ge(m_copied, k)
                    for e in range(2):
                        mm = nc.tensor.matmul(ps_hid[e], wa[:, :], cat_t[0:F, e * HALF:(e + 1) * HALF],
                                              start=True, stop=True)
                    mm.then_inc(m_hid, 1)
                    pe.wait_ge(m_relu, k)
                    if mode or not (isinstance(g, int) and g == 0):
                        pe.wait_ge(m_done, g + mode * STEPS)
                    for t in range(SW):
                        mm = nc.tensor.matmul(ps_node[:, t * D:(t + 1) * D], hid[:, t * P:(t + 1) * P],
                                              wb[:, :], start=True, stop=True)
                    mm.then_inc(m_node, 1)
                paired(pe, STEPS, step)

            pe.wait_ge(s_w, WLOAD)
            for mode in range(3):
                turn(mode)
                if mode < 2:
                    node_step(mode)

        @block.vector
        def _(dve):
            V = nc.vector
            V.memset(xs[:, W - 1, :], 0.0)
            V.memset(dst_side[:, :], -1).then_inc(s_xpad, 1)
            V.memset(ones[:, :], 1.0)
            V.memset(zeros_b[:, :], 0.0)
            V.memset(nothing[0][:, :, 0:A], 0.0)
            V.memset(nothing[0][:, :, A:D], -BIG)
            V.memset(nothing[1][:, :, :], 0.0)
            V.memset(carry_t[:, 0:1], 0.0)
            V.memset(sentinel[:, :], -1.0).then_inc(s_keep, 1)
            dve.wait_ge(s_iota, 2)
            for t in (ident, ident_b):
                V.tensor_scalar(t[:, :], diff[:, :], 0.0, None, ALU.is_equal)
            for t in (before, before_b):
                V.tensor_scalar(t[:, :], diff[:, :], 0.0, None, ALU.is_gt)
            V.tensor_copy(col[:, :], col_i[:, :]).then_inc(s_const, 1)
            dve.wait_ge(s_const, 1)
            dve.wait_ge(s_src, 16)
            V.tensor_scalar(part[0], src_i[:, :], P - 1, None, ALU.bitwise_and).then_inc(s_part, 1)
            V.tensor_scalar(part[1], src_i[:, :], 7, None, ALU.logical_shift_right).then_inc(s_part, 1)
            dve.wait_ge(s_dst, 48)
            V.tensor_scalar(part[2], dst_i, P - 1, None, ALU.bitwise_and).then_inc(s_part, 1)
            V.tensor_scalar(part[3], dst_i, 7, None, ALU.logical_shift_right).then_inc(s_part, 1)
            V.tensor_copy(edge_key[1][:, 0:1], dst_i[:, 0:1])
            V.tensor_copy(edge_key[1][:, 1:2], dst_i[:, COLS - 1:COLS])
            V.tensor_copy(edge_key[1][:, 2:3], dst_side[:, 1:2])
            V.tensor_tensor(cont[:, 0:1], dst_i[:, 0:1], dst_side[:, 0:1], ALU.is_equal)
            V.tensor_tensor(cont[:, 1:COLS], dst_i[:, 1:COLS], dst_i[:, 0:COLS - 1],
                            ALU.is_equal).then_inc(s_const, 1)
            dve.wait_ge(s_keys, 4)

            def onehots(g, h, staged, outs, used):
                if not at_start(g):
                    dve.wait_ge(used, g - 1)
                V.tensor_copy(stage_f[h][:, :, :], keys[:, bass.ds(g * GT, GT), :]).then_inc(staged, 1)
                dve.wait_ge(staged, g + 1)
                for k, o, n in outs:
                    for t in range(GT):
                        op = V.tensor_scalar(o[h][:, t, :], col[:, 0:n], stage_f[h][:, t, k:k + 1], None,
                                             ALU.is_equal)
                return op

            def count(g, h, i):
                onehots(g, h, a_staged, ((0, lo, P), (1, hi, W)), a_used).then_inc(a_onehot, 1)

            paired(dve, GROUPS, count)

            chain = [0]

            def link(op):
                chain[0] += 1
                op.then_inc(n_chain, 1)
                dve.wait_ge(n_chain, chain[0])

            def prefix(k, counts):
                V.tensor_copy(cnt[k][:, :], counts).then_inc(n_cnt, 1)
                dve.wait_ge(n_cnt, k + 1)
                dve.wait_ge(n_sums, k + 1)
                link(V.tensor_copy(total[:, :], ps_small[1]))
                link(V.tensor_tensor_scan(incl[:, :], ones[:, 0:W], total[:, :], 0.0, ALU.mult, ALU.add))
                link(V.tensor_tensor(incl[:, :], incl[:, :], total[:, :], ALU.subtract))
                link(V.tensor_tensor(base[:, :], incl[:, :], ps_small[0], ALU.add))
                link(V.tensor_scalar(has[:, :], cnt[k][:, :], 0.0, None, ALU.is_gt))
                link(V.tensor_tensor(last[:, :], base[:, :], cnt[k][:, :], ALU.add))
                link(V.scalar_tensor_tensor(last[:, :], last[:, :], float(-1 - E), has[:, :], ALU.add, ALU.mult))
                link(V.tensor_scalar(end_row[k][:, :], last[:, :], float(E), None, ALU.add))

            dve.wait_ge(a_used, GROUPS)
            prefix(0, ps_src)
            V.tensor_scalar(base[:, :], base[:, :], 1.0, None, ALU.add).then_inc(n_seed, 1)
            link(V.tensor_scalar(inv_cnt[:, :], cnt[0][:, :], 1.0, None, ALU.max))
            link(V.reciprocal(inv_cnt[:, :], inv_cnt[:, :]))

            def rank_onehots(g, h):
                onehots(g, h, b_staged, ((0, lo, P), (1, hi, W), (2, dlo, P), (3, dhi, W)),
                        b_picked).then_inc(b_onehot, 1)

            def place(g, h, i):
                if not at_end(g, GROUPS):
                    rank_onehots(g + 1, 1 - h)
                dve.wait_ge(b_same, g + 1)
                V.tensor_tensor(same[:, :, :], ps_same.rearrange("p (t e) -> p t e", e=P),
                                before_b[:, :].unsqueeze(1).to_broadcast([P, GT, P]),
                                ALU.mult).then_inc(b_masked, 1)
                dve.wait_ge(b_ranked, g + 1)
                V.tensor_tensor(picked[:, :, :], ps_rank[h].rearrange("p (t w) -> p t w", w=W),
                                hi[h][:, :, :], ALU.mult).then_inc(b_picked, 1)
                dve.wait_ge(b_picked, g + 1)
                dve.wait_ge(b_rows, g + 1)
                V.tensor_reduce(rank[h][:, :], picked[:, :, :], AX, ALU.add).then_inc(b_pos, 1)

            rank_onehots(0, 0)
            paired(dve, GROUPS, place)

            dve.wait_ge(b_ranked, GROUPS)
            prefix(1, ps_dst)
            V.tensor_scalar(last[:, :], cnt[1][:, :], 1.0, None, ALU.add).then_inc(n_deg, 1)
            dve.wait_ge(n_root, 1)
            link(V.reciprocal(dis[:, :], root[:, :]))
            dve.wait_ge(s_x, 32)
            dve.wait_ge(s_w, WLOAD)
            link(V.tensor_tensor(xs[:, :, :], xs[:, :, :], b2_s[:, :].unsqueeze(1).to_broadcast([P, W, D]),
                                 ALU.add))
            link(V.scalar_tensor_tensor(bias0[:, :], bcol[:, 1:2], bcol[:, 2:3], bcol[:, 0:1],
                                        ALU.mult, ALU.add))

            def scan(g, h, i):
                dve.wait_ge(c_in[h], i * 32 + 32)
                if not (isinstance(g, int) and g == 0):
                    dve.wait_ge(c_scan, g)
                e = scan_in[h].rearrange("p (j f) -> p j f", f=ROW)
                V.tensor_tensor(flag[:, :], e[:, 1:SJ + 1, A], e[:, 0:SJ, A], ALU.is_equal).then_inc(c_flag, 1)
                dve.wait_ge(c_flag, g * 3 + 1)
                V.tensor_reduce(whole_c[:, bass.ds(g, 1)], flag[:, :], AX, ALU.min)
                V.tensor_scalar(sign[:, :], flag[:, :], 2.0, -1.0, ALU.mult, ALU.add).then_inc(c_flag, 1)
                if isinstance(g, int) and g == 0:
                    V.tensor_copy(first_cont[0][:, :], flag[:, 0:1])
                    V.tensor_copy(edge_key[0][:, 0:1], e[:, 1, A:A + 1])
                if at_end(g, SCHUNKS):
                    V.tensor_copy(edge_key[0][:, 1:2], e[:, SJ, A:A + 1])
                dve.wait_ge(c_flag, g * 3 + 2)
                V.tensor_scalar(limit[:, :], sign[:, :], BIG, None, ALU.mult).then_inc(c_flag, 1)
                dve.wait_ge(c_flag, g * 3 + 3)
                if not at_start(g):
                    dve.wait_ge(c_out[h], i * 16)
                for f in range(A):
                    for at, ctl, op0, op1, none in ((f, flag, ALU.mult, ALU.add, 0.0),
                                                    (A + f, limit, ALU.min, ALU.max, -BIG)):
                        before_it = none if isinstance(g, int) and g == 0 else scan_out[1 - h][:, SJ - 1, at:at + 1]
                        op = V.tensor_tensor_scan(scan_out[h][:, :, at], ctl[:, :], e[:, 1:SJ + 1, f],
                                                  before_it, op0, op1)
                op.then_inc(c_scan, 1)

            paired(dve, SCHUNKS, scan)

            def carries(mode):
                base_k, step = 8 * mode, [0]
                k = min(mode, 1)

                def klink(op):
                    step[0] += 1
                    op.then_inc(k_chain, 1)
                    dve.wait_ge(k_chain, base_k + step[0])

                if mode == 0:
                    dve.wait_ge(c_scan, SCHUNKS)
                    klink(V.tensor_reduce(whole[0][:, :], whole_c[:, :], AX, ALU.min))
                    dve.wait_ge(c_next, 16)
                else:
                    dve.wait_ge(g_chain, mode * LINKS)
                    klink(V.tensor_reduce(whole[1][:, :], cont[:, :], AX, ALU.min))
                klink(V.tensor_copy(whole_w[:, :], whole[k][:, 0:1].to_broadcast([P, D])))
                dve.wait_ge(k_turned, mode + 1)
                klink(V.tensor_copy(turned[:, :], ps_turn[0:D, 0:2 * P]))
                klink(V.tensor_scalar(sign_t[:, :], turned[:, 0:P], 2.0, -1.0, ALU.mult, ALU.add))
                klink(V.tensor_scalar(limit_t[:, :], sign_t[:, :], BIG, None, ALU.mult))
                S = A if mode == 0 else D
                klink(V.tensor_tensor_scan(carry_t[0:S, 1:P + 1], turned[0:S, 0:P], turned[0:S, P:2 * P],
                                           0.0, ALU.mult, ALU.add))
                if mode == 0:
                    klink(V.tensor_tensor_scan(carry_t[A:D, 1:P + 1], limit_t[A:D, :], turned[A:D, P:2 * P],
                                               -BIG, ALU.min, ALU.max))
                else:
                    klink(V.memset(carry_t[:, 0:1], 0.0))
                f0 = first_cont[0][:, :] if mode == 0 else cont[:, 0:1]
                key = edge_key[k]
                if mode < 2:
                    link(V.tensor_tensor(work[:, 0:1], key[:, 1:2], key[:, 2:3], ALU.is_equal))
                    link(V.tensor_tensor(work[:, 1:2], work[:, 0:1], whole[k][:, :], ALU.mult))
                    link(V.tensor_scalar(work[:, 2:3], work[:, 1:2], -1.0, 1.0, ALU.mult, ALU.add))
                    link(V.tensor_tensor(work[:, 0:1], work[:, 2:3], f0, ALU.mult))
                    link(V.scalar_tensor_tensor(work[:, 1:2], key[:, 0:1], float(-NPAD), work[:, 0:1],
                                                ALU.add, ALU.mult))
                    link(V.tensor_scalar(target[k][:, :], work[:, 1:2], float(NPAD), None, ALU.add))
                dve.wait_ge(k_back, mode + 1)
                klink(V.tensor_copy(carry[:, :], ps_turn[:, 2 * P:2 * P + D]))


            def node_stage(mode):
                def window(t, g):
                    return t[:, bass.ds(g * SW, SW), :]

                def wide(t, g, n):
                    return t[:, bass.ds(g * SW, SW)].unsqueeze(2).to_broadcast([P, SW, n])

                def features(g, h, i):
                    step = [0]

                    def mlink(op):
                        step[0] += 1
                        op.then_inc(m_link, 1)
                        dve.wait_ge(m_link, g * 2 + (2 * mode * STEPS + step[0]))

                    for k in range(SW):
                        dve.wait_ge(m_got[h][k], i * 16 + 16 * (mode * STEPS // 2 + 1))
                    dve.wait_ge(m_corr[h], i * 16 + 16 * (mode * STEPS // 2 + 1))
                    c = cat[h]
                    if mode == 0:
                        mlink(V.tensor_tensor(c[:, :, 0:A], window(agg, g)[:, :, 0:A], corr[h][:, :, 0:A], ALU.add))
                        mlink(V.tensor_tensor(c[:, :, A:D], window(agg, g)[:, :, A:D], corr[h][:, :, A:D], ALU.max))
                        V.tensor_tensor(c[:, :, D:3 * A], c[:, :, 0:A], wide(inv_cnt, g, A),
                                        ALU.mult).then_inc(m_cat, 1)
                    else:
                        dve.wait_ge(m_cat, g + mode * STEPS)
                        mlink(V.tensor_tensor(sq[:, :, :], window(agg, g), corr[h][:, :, :], ALU.add))
                        mlink(V.tensor_tensor(sq[:, :, :], sq[:, :, :], window(ys, g), ALU.add))
                        V.tensor_tensor(c[:, :, 0:D], sq[:, :, :], wide(dis, g, D), ALU.mult).then_inc(m_cat, 1)

                def result(g, h, i):
                    if mode == 1:
                        dve.wait_ge(m_node, g + (STEPS + 1))
                        V.tensor_tensor(window(ys, g), ps_node.rearrange("p (t f) -> p t f", f=D),
                                        wide(dis, g, D), ALU.mult).then_inc(m_done, 1)
                        return
                    step = [0]
                    first = 0 if mode == 0 else 7 * STEPS

                    def clink(op):
                        step[0] += 1
                        op.then_inc(m_chain, 1)
                        dve.wait_ge(m_chain, g * 7 + (first + step[0]))

                    def spread(k):
                        return stat[:, k, :].unsqueeze(2).to_broadcast([P, SW, D])

                    if mode == 0:
                        dve.wait_ge(m_node, g + 1)
                        clink(V.tensor_tensor(mid[:, :, :], ps_node.rearrange("p (t f) -> p t f", f=D),
                                              window(xs, g), ALU.add))
                    else:
                        dve.wait_ge(m_cat, g + (2 * STEPS + 1))
                        dve.wait_ge(m_done, g + 2 * STEPS)
                        clink(V.tensor_tensor(mid[:, :, :], cat[h][:, :, 0:D], window(xs, g), ALU.add))
                    clink(V.tensor_reduce(stat[:, 0, :], mid[:, :, :], AX, ALU.add))
                    clink(V.tensor_scalar(stat[:, 0, :], stat[:, 0, :], -1.0 / D, None, ALU.mult))
                    clink(V.tensor_tensor(mid[:, :, :], mid[:, :, :], spread(0), ALU.add))
                    clink(V.tensor_tensor(sq[:, :, :], mid[:, :, :], mid[:, :, :], ALU.mult))
                    clink(V.tensor_reduce(stat[:, 0, :], sq[:, :, :], AX, ALU.add))
                    V.tensor_scalar(stat[:, 1, :], stat[:, 0, :], 1.0 / D, EPS, ALU.mult, ALU.add).then_inc(m_var, 1)
                    dve.wait_ge(m_root, g + (mode // 2 * STEPS + 1))
                    clink(V.reciprocal(stat[:, 3, :], stat[:, 2, :]))
                    if mode == 0:
                        V.tensor_tensor(res[0][:, :, :], mid[:, :, :], spread(3), ALU.mult).then_inc(s_xready, 1)
                        dve.wait_ge(s_xready, g + 1)
                        V.tensor_tensor(window(xs, g), res[0][:, :, :],
                                        c2_s[:, :].unsqueeze(1).to_broadcast([P, SW, D]), ALU.add)
                        V.tensor_tensor(window(ys, g), res[0][:, :, :], wide(dis, g, D),
                                        ALU.mult).then_inc(m_done, 1)
                    else:
                        if not at_start(g):
                            dve.wait_ge(m_store[h], i * 16 + 16 * STEPS)
                        V.tensor_tensor(res[h][:, :, :], mid[:, :, :], spread(3), ALU.mult).then_inc(m_done, 1)

                features(0, 0, 0)

                def body(g, h, i):
                    features(g + 1, 1 - h, i + h)
                    result(g, h, i)
                paired(dve, STEPS - 1, body)
                result(STEPS - 1, 1, STEPS // 2 - 1)

            carries(0)
            node_stage(0)
            for q in range(2):
                def add_up(g, h, i):
                    if not at_start(g):
                        dve.wait_ge(g_chain, g * CJ + (q * LINKS - CJ - 1))
                    V.tensor_copy(gflag[h][:, :], cont[:, bass.ds(g * CJ, CJ)]).then_inc(g_flag, 1)
                    dve.wait_ge(g_flag, g + (q * CHUNKS + 1))
                    for j in range(CJ):
                        dve.wait_ge(g_got[h][j], i * 16 + (16 * q * G_HALF[h] + 16))
                        if isinstance(g, int) and g == 0 and j == 0:
                            continue
                        if not (isinstance(g, int) and g == 0 and j == 1 and q == 0):
                            dve.wait_ge(g_chain, g * CJ + (q * LINKS + j - 1))
                        prior = got_rows[h][:, j - 1, :] if j else got_rows[1 - h][:, CJ - 1, :]
                        V.scalar_tensor_tensor(got_rows[h][:, j, :], prior, gflag[h][:, j:j + 1],
                                               got_rows[h][:, j, :], ALU.mult, ALU.add).then_inc(g_chain, 1)
                paired(dve, CHUNKS, add_up)
                carries(q + 1)
                node_stage(q + 1)


_INS = ["x", "src", "dst", "edge_attr_32", "L0_gnn_u", "L0_gnn_W1", "L0_gnn_b1", "L0_gnn_W2", "L0_gnn_b2",
        "L1_gnn_W1", "L1_gnn_b1", "L1_gnn_W2", "L1_gnn_b2"]


def kernel(**inputs):
    import numpy as np
    import concourse.bacc as bacc
    from concourse.bass_utils import run_bass_kernel_spmd as run

    nc = bacc.Bacc("TRN2", target_bir_lowering=False, num_devices=1)
    arrays, args = {}, []
    for name in _INS:
        a = np.ascontiguousarray(inputs[name])
        arrays[f"in_{name}"] = a
        args.append(nc.dram_tensor(f"in_{name}", a.shape, mybir.dt.from_np(a.dtype), kind="ExternalInput").ap())
    result = nc.dram_tensor("result", (N, D), F32, kind="ExternalOutput").ap()
    build(nc, *args, result)
    r = run(nc, [arrays], core_ids=[0])
    return r.results[0]["result"]
```

```python
from contextlib import ExitStack

import concourse.bass as bass
from concourse import mybir

F32, BF16, I32 = mybir.dt.float32, mybir.dt.bfloat16, mybir.dt.int32
ALU = mybir.AluOpType
ACT = mybir.ActivationFunctionType
AX = mybir.AxisListType.X

P = 128
N, E = 12500, 400000
COLS = E // P
W = -(-N // P)
NPAD = W * P
LASTROWS = N - (W - 1) * P
D, A, HID = 64, 32, 128
ROW = A + 1
GT = 5
GROUPS = COLS // GT
UT = 2 * GT
UNITS = -(-COLS // UT)
SJ = 125
SCHUNKS = COLS // SJ
CJ = 25
CHUNKS = COLS // CJ
SW = 7
STEPS = W // SW
BIG = 3.4e38
EPS = 1e-5
assert E % P == 0 and GROUPS * GT == COLS and GROUPS % 2 and UNITS % 2 and SCHUNKS % 2 and CHUNKS % 2 and STEPS * SW == W


def paired(eng, count, body):
    pairs = count // 2
    body(0, 0, 0)
    body(1, 1, 0)
    with eng.Fori(1, pairs) as i:
        body(i * 2, 0, i)
        body(i * 2 + 1, 1, i)
    if count % 2:
        body(count - 1, 0, pairs)


def build(nc, x, src, dst, attr, u, w1, b1, w2, b2, v1, c1, v2, c2, out):
    with ExitStack() as ctx:
        def sb(name, shape, dt=F32):
            return ctx.enter_context(nc.sbuf_tensor(name, shape, dt))

        def pair(name, shape, dt=F32):
            return [sb(f"{name}{h}", shape, dt) for h in range(2)]

        def sem(name):
            return ctx.enter_context(nc.semaphore(name))

        def dram(name, shape):
            return nc.dram_tensor(name, shape, F32, kind="Internal").ap()

        by_src = dram("by_src", (E + 2, ROW))
        running = [dram(f"running{k}", (E + 1, D)) for k in range(3)]
        correction = [dram(f"correction{k}", (NPAD, D)) for k in range(3)]
        table = [dram(f"table{k}", (NPAD, D)) for k in range(2)]

        def node_view(t):
            return t.rearrange("(w l) f -> l w f", l=P)

        def edge_view(t, first=0):
            return t[first:first + E, :].rearrange("(p j) f -> p (j f)", p=P)

        ps = ctx.enter_context(nc.psum_tensor("ps", [P, 8 * 512], F32))
        ps_src = ps[:, 0:W]
        ps_dst = ps[:, 512:512 + W]
        ps_small = [ps[:, 1024:1024 + W], ps[:, 1024 + P:1024 + P + W]]
        ps_lot = ps[:, 1024:1024 + GT * P // 2].bitcast(BF16)
        ps_same = ps[:, 1536:1536 + GT * P]
        ps_rank = [ps[:, 2560 + 512 * h:2560 + 512 * h + GT * W] for h in range(2)]
        HALF = SW * P // 2
        ps_cat = ps[:, 1536:1536 + SW * P]
        ps_hid = [ps[:, 2560 + 512 * h:2560 + 512 * h + HALF] for h in range(2)]
        ps_node = ps[:, 3584:3584 + SW * D]
        ps_turn = ps[:, 0:512]

        diff = sb("diff", [P, P], I32)
        col = sb("col", [P, P, UT], BF16)
        ident = sb("ident", [P, P])
        ident_b = sb("ident_b", [P, P], BF16)
        before = sb("before", [P, P])
        before_b = sb("before_b", [P, P], BF16)
        ones = sb("ones", [P, P])
        zeros_b = sb("zeros_b", [P, P], BF16)
        nothing = pair("nothing", [P, SW, D])
        sentinel = sb("sentinel", [P, D])

        arena = sb("arena", [P, 2 * SJ * D])
        scan_out = [arena[:, h * SJ * D:(h + 1) * SJ * D].rearrange("p (j f) -> p j f", f=D) for h in range(2)]
        agg = arena[:, 0:W * D].rearrange("p (w f) -> p w f", f=D)
        ys = arena[:, SJ * D:SJ * D + W * D].rearrange("p (w f) -> p w f", f=D)
        dst_i = arena[:, 0:COLS].bitcast(I32)
        part = [arena[:, (k + 1) * COLS:(k + 2) * COLS].bitcast(I32) for k in range(4)]
        INLEN = (SJ + 1) * ROW
        arena2 = sb("arena2", [P, 2 * INLEN])
        KP = UNITS * UT
        keys = arena2[:, 0:2 * KP].bitcast(BF16).rearrange("p (k j) -> p k j", k=4)
        col_i = arena2[:, 2 * KP:2 * KP + P * UT].bitcast(I32)
        scan_in = [arena2[:, h * INLEN:(h + 1) * INLEN] for h in range(2)]
        got_rows = [arena2[:, h * CJ * D:(h + 1) * CJ * D].rearrange("p (j f) -> p j f", f=D) for h in range(2)]

        src_i = sb("src_i", [P, COLS], I32)
        cont = sb("cont", [P, COLS])

        lo = pair("lo", [P, P, UT], BF16)
        hi = pair("hi", [P, W, UT], BF16)
        dlo = pair("dlo", [P, P, UT], BF16)
        dhi = pair("dhi", [P, W, UT], BF16)
        lot_b = pair("lot_b", [P, GT * P], BF16)
        lot_f = pair("lot_f", [P, GT * P])
        same = pair("same", [P, GT, P], BF16)
        snap = pair("snap", [P, W])
        picked = sb("picked", [P, GT, W])
        rank = [pair(f"rank{b}", [P, GT], I32) for b in range(2)]
        attr_in = pair("attr_in", [P, GT, A])
        rows = [pair(f"rows{b}", [P, GT, ROW]) for b in range(2)]

        flag = sb("flag", [P, SJ])
        sign = sb("sign", [P, SJ])
        limit = sb("limit", [P, SJ])
        whole_c = sb("whole_c", [P, SCHUNKS])
        gflag = pair("gflag", [P, CJ])
        gidx = pair("gidx", [P, CJ], I32)

        cnt = pair("cnt", [P, W])
        total = sb("total", [P, W])
        incl = sb("incl", [P, W])
        base = sb("base", [P, W])
        has = sb("has", [P, W])
        last = sb("last", [P, W])
        end_row = pair("end_row", [P, W], I32)
        inv_cnt = sb("inv_cnt", [P, W])
        root = sb("root", [P, W])
        dis = sb("dis", [P, W])
        xs = sb("xs", [P, W, D])
        corr = pair("corr", [P, SW, D])
        NODE = 2 * CJ * D
        cat_t = arena2[0:3 * A, NODE:NODE + SW * P]
        hid = arena2[:, NODE + SW * P:NODE + 2 * SW * P]
        mid, sq, *res = (arena2[:, NODE + 2 * SW * P + k * SW * D:NODE + 2 * SW * P + (k + 1) * SW * D]
                         .rearrange("p (w f) -> p w f", f=D) for k in range(4))
        stat = sb("stat", [P, 4, SW])

        CAT = NODE + 2 * SW * P + 4 * SW * D
        cat = [arena2[:, CAT + h * SW * 3 * A:CAT + (h + 1) * SW * 3 * A].rearrange("p (w f) -> p w f", f=3 * A)
               for h in range(2)]

        whole = pair("whole", [P, 1])
        edge_key = [sb(f"edge_key{k}", [P, 3]) for k in range(2)]
        first_cont = pair("first_cont", [P, 1])
        dst_side = sb("dst_side", [P, 2], I32)
        work = sb("work", [P, 4])
        target = pair("target", [P, 1], I32)
        whole_w = sb("whole_w", [P, D])
        turned = sb("turned", [D, 2 * P])
        sign_t = sb("sign_t", [D, P])
        limit_t = sb("limit_t", [D, P])
        carry_t = sb("carry_t", [D, P + 1])
        carry = sb("carry", [P, D])

        w1_s = sb("w1_s", [3 * A, HID])
        w2_s = sb("w2_s", [HID, D])
        v1_s = sb("v1_s", [D, HID])
        v2_s = sb("v2_s", [HID, D])
        bcol = sb("bcol", [P, 4])
        bias0 = sb("bias0", [P, 1])
        b2_s = sb("b2_s", [P, D])
        c2_s = sb("c2_s", [P, D])

        s_src, s_dst, s_x, s_w, s_iota, s_const, s_init, s_keep = (sem(n) for n in (
            "s_src", "s_dst", "s_x", "s_w", "s_iota", "s_const", "s_init", "s_keep"))
        s_part, s_keys, s_xready, s_xpad = (sem(n) for n in ("s_part", "s_keys", "s_xready", "s_xpad"))
        a_onehot, a_used = (sem(n) for n in ("a_onehot", "a_used"))
        n_cnt, n_sums, n_chain, n_seed, n_deg, n_root = (sem(n) for n in (
            "n_cnt", "n_sums", "n_chain", "n_seed", "n_deg", "n_root"))
        b_onehot, b_turned, b_copied, b_same, b_masked = (sem(n) for n in (
            "b_onehot", "b_turned", "b_copied", "b_same", "b_masked"))
        b_snap, b_state, b_looked, b_ranked, b_picked, b_pos, b_rows, b_seen = (sem(n) for n in (
            "b_snap", "b_state", "b_looked", "b_ranked", "b_picked", "b_pos", "b_rows", "b_seen"))
        b_attr = [sem(f"b_attr{h}") for h in range(2)]
        b_scat = [[[sem(f"b_scat{b}{h}_{k}") for k in range(GT)] for h in range(2)] for b in range(2)]
        c_in = [sem(f"c_in{h}") for h in range(2)]
        c_out = [sem(f"c_out{h}") for h in range(2)]
        c_next, c_flag, c_scan = sem("c_next"), sem("c_flag"), sem("c_scan")
        g_staged, g_seen, g_flag, g_chain = (sem(n) for n in (
            "g_staged", "g_seen", "g_flag", "g_chain"))
        g_got = [[sem(f"g_got{h}_{k}") for k in range(CJ)] for h in range(2)]
        g_out = [sem(f"g_out{h}") for h in range(2)]
        k_chain, k_turned, k_back, k_scat = (sem(n) for n in (
            "k_chain", "k_turned", "k_back", "k_scat"))
        m_got = [[sem(f"m_got{h}_{k}") for k in range(SW)] for h in range(2)]
        m_corr = [sem(f"m_corr{h}") for h in range(2)]
        m_link, m_cat, m_turned, m_copied, m_hid, m_relu, m_node, m_chain, m_var, m_root, m_done = (
            sem(n) for n in ("m_link", "m_cat", "m_turned", "m_copied", "m_hid", "m_relu", "m_node",
                             "m_chain", "m_var", "m_root", "m_done"))
        m_store = [sem(f"m_store{h}") for h in range(2)]
        ctx.enter_context(nc.allow_non_contiguous_dma(reason="columns of 128 numbers"))
        ctx.enter_context(nc.allow_low_precision(reason="a sum with one term that isn't zero, a whole number"))
        block = ctx.enter_context(nc.Block())

        G_HALF = [CHUNKS - CHUNKS // 2, CHUNKS // 2]
        C_HALF = [SCHUNKS - SCHUNKS // 2, SCHUNKS // 2]
        LINKS = COLS - 1
        INIT = 16 * (3 * STEPS + 3 + 2)
        WLOAD = 16 * 10

        def at_end(g, count):
            return isinstance(g, int) and g == count - 1

        def at_start(g):
            return isinstance(g, int) and g < 2

        @block.sync
        def _(sp):
            sp.dma_start(src_i[:, :], src.rearrange("(p j) -> p j", p=P)).then_inc(s_src, 16)
            sp.dma_start(dst_i, dst.rearrange("(p j) -> p j", p=P)).then_inc(s_dst, 16)
            sp.wait_ge(s_xpad, 1)
            dst_rows = dst.rearrange("(p j a) -> p j a", p=P, a=1)
            sp.dma_start(dst_side[1:P, 0:1], dst_rows[0:P - 1, COLS - 1, :]).then_inc(s_dst, 16)
            sp.dma_start(dst_side[0:P - 1, 1:2], dst_rows[1:P, 0, :]).then_inc(s_dst, 16)
            sp.dma_start(xs[:, 0:W - 1, :],
                         x[0:(W - 1) * P, :].rearrange("(w l) f -> l w f", l=P)).then_inc(s_x, 16)
            sp.dma_start(xs[0:LASTROWS, W - 1, :], x[(W - 1) * P:N, :]).then_inc(s_x, 16)
            for to, frm in ((w1_s[:, :], w1[0:3 * A, :]), (w2_s[:, :], w2), (v1_s[:, :], v1), (v2_s[:, :], v2),
                            (bcol[:, 0:1], b1.rearrange("(p a) -> p a", a=1)),
                            (bcol[:, 1:2], w1[3 * A:3 * A + 1, :].rearrange("a p -> p a")),
                            (bcol[:, 2:3], u[0:1, 0:1].to_broadcast([P, 1])),
                            (bcol[:, 3:4], c1.rearrange("(p a) -> p a", a=1)),
                            (b2_s[:, :], b2.rearrange("(a f) -> a f", a=1).to_broadcast([P, D])),
                            (c2_s[:, :], c2.rearrange("(a f) -> a f", a=1).to_broadcast([P, D]))):
                sp.dma_start(to, frm).then_inc(s_w, 16)
            sp.wait_ge(s_keep, 1)
            for k in range(3):
                sp.dma_start(running[k][E:E + 1, :], nothing[1][0:1, 0, :]).then_inc(s_init, 16)
            sp.dma_start(by_src[0:1, :], sentinel[0:1, 0:ROW]).then_inc(s_init, 16)
            sp.dma_start(by_src[E + 1:E + 2, :], sentinel[0:1, 0:ROW]).then_inc(s_init, 16)
            with sp.Fori(0, STEPS) as s:
                for k in range(3):
                    sp.dma_start(node_view(correction[k])[:, bass.ds(s * SW, SW), :],
                                 nothing[min(k, 1)][:, :, :]).then_inc(s_init, 16)

            def attributes(g, h, i):
                if not at_start(g):
                    sp.wait_ge(b_rows, g - 1)
                sp.dma_start(attr_in[h].rearrange("p t a -> p (t a)"),
                             edge_view(attr)[:, bass.ds(g * (GT * A), GT * A)]).then_inc(b_attr[h], 16)

            paired(sp, GROUPS, attributes)

            for b in range(2):
                for h in range(2):
                    for k in range(GT):
                        sp.wait_ge(b_scat[b][h][k], 16 * len(range(2 * b + h, GROUPS, 4)))
            sp.wait_ge(s_init, INIT)
            sp.dma_start(edge_key[0][:, 2:3], by_src[2:E + 2, :].rearrange("(p j) f -> p j f", p=P)[
                :, COLS - 1, A:A + 1]).then_inc(c_next, 16)

            def scan_load(g, h, i):
                if not at_start(g):
                    sp.wait_ge(c_scan, g - 1)
                sp.dma_start(scan_in[h][:, 0:ROW],
                             edge_view(by_src)[:, bass.ds(g * (SJ * ROW), ROW)]).then_inc(c_in[h], 16)
                sp.dma_start(scan_in[h][:, ROW:INLEN],
                             edge_view(by_src, 1)[:, bass.ds(g * (SJ * ROW), SJ * ROW)]).then_inc(c_in[h], 16)

            paired(sp, SCHUNKS, scan_load)

            def step_load(mode):
                def load(g, h, i):
                    if mode or not at_start(g):
                        sp.wait_ge(m_cat, mode * STEPS + g - 1)
                    sp.dma_start(corr[h][:, :, :],
                                 node_view(correction[mode])[:, bass.ds(g * SW, SW), :]).then_inc(m_corr[h], 16)
                return load

            def step_store(mode):
                def store(g, h, i):
                    sp.wait_ge(m_done, mode * STEPS + g + 1)
                    if mode < 2:
                        sp.dma_start(node_view(table[mode])[:, bass.ds(g * SW, SW), :],
                                     ys[:, bass.ds(g * SW, SW), :]).then_inc(m_store[h], 16)
                    elif at_end(g, STEPS):
                        sp.dma_start(out[g * SW * P:(W - 1) * P, :].rearrange("(w l) f -> l w f", l=P),
                                     res[h][:, 0:SW - 1, :]).then_inc(m_store[h], 16)
                        sp.dma_start(out[(W - 1) * P:N, :], res[h][0:LASTROWS, SW - 1, :]).then_inc(m_store[h], 16)
                    else:
                        sp.dma_start(out[0:(W - 1) * P, :].rearrange("(w l) f -> l w f", l=P)[
                            :, bass.ds(g * SW, SW), :], res[h][:, :, :]).then_inc(m_store[h], 16)
                return store

            def node_io(mode):
                sp.wait_ge(k_scat, 16 * (mode + 1))
                load, store = step_load(mode), step_store(mode)
                load(0, 0, 0)

                def body(g, h, i):
                    load(g + 1, 1 - h, 0)
                    store(g, h, i)
                paired(sp, STEPS - 1, body)
                store(STEPS - 1, 1, 0)

            node_io(0)
            for q in range(2):
                def rows_out(g, h, i):
                    sp.wait_ge(g_chain, g * CJ + (q * LINKS + CJ - 1))
                    sp.dma_start(edge_view(running[q + 1])[:, bass.ds(g * (CJ * D), CJ * D)],
                                 got_rows[h].rearrange("p j f -> p (j f)")).then_inc(g_out[h], 16)
                paired(sp, CHUNKS, rows_out)
                node_io(q + 1)
            for h in range(2):
                sp.wait_ge(m_store[h], 16 * (3 * STEPS // 2 + h))

        @block.gpsimd
        def _(pool):
            nc.gpsimd.iota(diff[:, :], [[1, P]], base=0, channel_multiplier=-1).then_inc(s_iota, 1)
            nc.gpsimd.iota(col_i, [[1, P], [0, UT]], base=0, channel_multiplier=0).then_inc(s_iota, 1)

            def scatter(v, b, i):
                for h in range(1 if at_end(v, UNITS) else 2):
                    pool.wait_ge(b_pos, v * 2 + (h + 1))
                    pool.sem_inc(b_seen, 1)
                    pool.wait_ge(b_rows, v * 2 + (h + 1))
                    pool.sem_inc(b_seen, 1)
                    for k in range(GT):
                        nc.gpsimd.indirect_dma_start(
                            out=by_src, out_offset=bass.IndirectOffsetOnAxis(ap=rank[b][h][:, k:k + 1], axis=0),
                            in_=rows[b][h][:, k, :], in_offset=None).then_inc(b_scat[b][h][k], 16)

            pool.wait_ge(s_init, INIT)
            paired(pool, UNITS, scatter)

            def aggregate(mode):
                pool.wait_ge(k_chain, 8 * mode + 8)
                nc.gpsimd.indirect_dma_start(
                    out=correction[mode],
                    out_offset=bass.IndirectOffsetOnAxis(ap=target[min(mode, 1)][:, 0:1], axis=0),
                    in_=carry[:, :], in_offset=None, bounds_check=NPAD - 1,
                    oob_is_err=False).then_inc(k_scat, 16)
                for h in range(2):
                    if mode == 0:
                        pool.wait_ge(c_out[h], 16 * C_HALF[h])
                    else:
                        pool.wait_ge(g_out[h], 16 * mode * G_HALF[h])
                if mode == 0:
                    pool.wait_ge(n_deg, 1)
                for w in range(W):
                    h, k, turn = w // SW % 2, w % SW, mode * STEPS // 2 + w // (2 * SW)
                    if turn:
                        pool.wait_ge(m_got[h][k], 16 * turn)
                    nc.gpsimd.indirect_dma_start(
                        out=agg[:, w, :], out_offset=None, in_=running[mode],
                        in_offset=bass.IndirectOffsetOnAxis(ap=end_row[min(mode, 1)][:, w:w + 1], axis=0),
                    ).then_inc(m_got[h][k], 16)

            aggregate(0)
            for q in range(2):
                for h in range(2):
                    pool.wait_ge(m_store[h], 16 * (q + 1) * (STEPS // 2))

                def gather(g, h, i):
                    pool.wait_ge(g_staged, g + (q * CHUNKS + 1))
                    pool.sem_inc(g_seen, 1)
                    if not at_start(g):
                        pool.wait_ge(g_out[h], i * 16 + 16 * q * G_HALF[h])
                        pool.sem_inc(g_seen, 1)
                        pool.wait_ge(g_chain, g * CJ + (q * LINKS - CJ))
                        pool.sem_inc(g_seen, 1)
                    for k in range(CJ):
                        nc.gpsimd.indirect_dma_start(
                            out=got_rows[h][:, k, :], out_offset=None, in_=table[q],
                            in_offset=bass.IndirectOffsetOnAxis(ap=gidx[h][:, k:k + 1], axis=0),
                            ).then_inc(g_got[h][k], 16)

                paired(pool, CHUNKS, gather)
                aggregate(q + 1)

        @block.scalar
        def _(act):
            def to_keys(k):
                act.wait_ge(s_part, k + 1)
                nc.scalar.copy(keys[:, k, 0:COLS], part[k]).then_inc(s_keys, 1)

            to_keys(0)
            to_keys(1)
            to_keys(2)
            to_keys(3)

            def copy_turned(g, h):
                act.wait_ge(b_turned, g + 1)
                nc.scalar.copy(lot_b[h][:, :], ps_lot)
                nc.scalar.copy(lot_f[h][:, :], ps_lot).then_inc(b_copied, 1)

            def snapshot(g, h, t):
                act.wait_ge(b_state, g * GT + (t + 1))
                if not (isinstance(g, int) and g * GT + t < 2):
                    act.wait_ge(b_looked, g * GT + (t - 1))
                nc.scalar.copy(snap[(h * GT + t) % 2][:, :], ps_src).then_inc(b_snap, 1)

            def unit(v, b, i):
                for h in range(1 if at_end(v, UNITS) else 2):
                    g = v * 2 + h
                    for t in range(GT):
                        snapshot(g, h, t)
                        if t == 0:
                            act.wait_ge(b_attr[h], v * 16 + 16)
                            if not at_start(v):
                                for k in range(GT):
                                    act.wait_ge(b_scat[b][h][k], i * 16)
                            nc.scalar.copy(rows[b][h][:, :, 0:A], attr_in[h][:, :, :])
                            nc.scalar.copy(rows[b][h][:, :, A], src_i[:, bass.ds(g * GT, GT)]).then_inc(b_rows, 1)
                        if t == 1 and not at_end(v, UNITS):
                            copy_turned(g + 1, 1 - h)

            copy_turned(0, 0)
            paired(act, UNITS, unit)

            act.wait_ge(n_deg, 1)
            nc.scalar.activation(root[:, :], last[:, :], ACT.Sqrt).then_inc(n_root, 1)

            def scan_store(g, h, i):
                act.wait_ge(c_scan, g + 1)
                act.dma_start(edge_view(running[0])[:, bass.ds(g * (SJ * D), SJ * D)],
                              scan_out[h].rearrange("p j f -> p (j f)")).then_inc(c_out[h], 16)

            paired(act, SCHUNKS, scan_store)

            def node_step(mode):
                F = D if mode else 3 * A
                bias = bcol[:, 3:4] if mode else bias0[:, 0:1]

                def step(g, h, i):
                    if mode < 2:
                        act.wait_ge(m_turned, g + (mode * STEPS + 1))
                        nc.scalar.copy(cat_t[0:F], ps_cat[0:F, :]).then_inc(m_copied, 1)
                        act.wait_ge(m_hid, g + (mode * STEPS + 1))
                        for e in range(2):
                            last_one = nc.scalar.activation(hid[:, e * HALF:(e + 1) * HALF], ps_hid[e],
                                                            ACT.Relu, bias=bias)
                        last_one.then_inc(m_relu, 1)
                    if mode != 1:
                        act.wait_ge(m_var, g + (mode // 2 * STEPS + 1))
                        nc.scalar.activation(stat[:, 2, :], stat[:, 1, :], ACT.Sqrt).then_inc(m_root, 1)
                paired(act, STEPS, step)

            node_step(0)
            for q in range(2):
                def stage_idx(g, h, i):
                    if q or not at_start(g):
                        act.wait_ge(g_chain, g * CJ + (q * LINKS - CJ - 1))
                    nc.scalar.copy(gidx[h][:, :], src_i[:, bass.ds(g * CJ, CJ)]).then_inc(g_staged, 1)
                paired(act, CHUNKS, stage_idx)
                node_step(q + 1)

        @block.tensor
        def _(pe):
            pe.wait_ge(s_const, 1)
            nc.tensor.matmul(ps_src, zeros_b[:, :], zeros_b[:, 0:W], start=True, stop=False,
                             skip_group_check=True)
            nc.tensor.matmul(ps_dst, zeros_b[:, :], zeros_b[:, 0:W], start=True, stop=False,
                             skip_group_check=True)

            def count(g, h, i):
                pe.wait_ge(a_onehot, g + 1)
                for t in range(UT if not at_end(g, UNITS) else COLS % UT):
                    mm = nc.tensor.matmul(ps_src, lo[h][:, :, t], hi[h][:, :, t], start=False, stop=False,
                                          skip_group_check=True)
                mm.then_inc(a_used, 1)

            paired(pe, UNITS, count)

            def prefix(k):
                pe.wait_ge(n_cnt, k + 1)
                nc.tensor.matmul(ps_small[0], before[:, :], cnt[k][:, :], start=True, stop=True)
                nc.tensor.matmul(ps_small[1], ones[:, :], cnt[k][:, :], start=True,
                                 stop=True).then_inc(n_sums, 1)

            prefix(0)
            pe.wait_ge(n_seed, 1)
            nc.tensor.matmul(ps_src, ident[:, :], base[:, :], start=True, stop=False,
                             skip_group_check=True).then_inc(b_state, 1)

            def turn_tiles(b, n, g, h, first):
                if not first:
                    pe.wait_ge(b_copied, g)
                for t in range(GT):
                    mm = nc.tensor.transpose(ps_lot[:, t * P:(t + 1) * P], lo[b][:, :, h * GT + t],
                                             ident_b[:, :])
                mm.then_inc(b_turned, 1)

            def pair_up(g, h, first):
                pe.wait_ge(b_copied, g + 1)
                if not first:
                    pe.wait_ge(b_masked, g)
                for t in range(GT):
                    one = lot_b[h][:, t * P:(t + 1) * P]
                    mm = nc.tensor.matmul(ps_same[:, t * P:(t + 1) * P], one, one, start=True, stop=True)
                mm.then_inc(b_same, 1)

            def look_up(b, g, h, t):
                k = h * GT + t
                pe.wait_ge(b_snap, g * GT + (t + 1))
                nc.tensor.matmul(ps_src, lo[b][:, :, k], hi[b][:, :, k], start=False, stop=False,
                                 skip_group_check=True).then_inc(b_state, 1)
                mm = nc.tensor.matmul(ps_rank[h][:, t * W:(t + 1) * W], lot_f[h][:, t * P:(t + 1) * P],
                                      snap[k % 2][:, :], start=(t == 0), stop=False, skip_group_check=True)
                mm.then_inc(b_looked, 1)

            def unit(v, b, i):
                for h in range(1 if at_end(v, UNITS) else 2):
                    g = v * 2 + h
                    more = not (at_end(v, UNITS))
                    if more:
                        if h == 1:
                            pe.wait_ge(b_onehot, v + 2)
                        turn_tiles(b if h == 0 else 1 - b, v, g + 1, 1 - h, False)
                    for t in range(GT):
                        if more and t == GT - 1:
                            pair_up(g + 1, 1 - h, False)
                        look_up(b, g, h, t)
                    for t in range(GT):
                        nc.tensor.matmul(ps_dst, dlo[b][:, :, h * GT + t], dhi[b][:, :, h * GT + t],
                                         start=False, stop=False, skip_group_check=True)
                    pe.wait_ge(b_masked, g + 1)
                    for t in range(GT):
                        mm = nc.tensor.matmul(ps_rank[h][:, t * W:(t + 1) * W], same[h][:, t, :],
                                              hi[b][:, :, h * GT + t], start=False, stop=(t == GT - 1),
                                              skip_group_check=True)
                    mm.then_inc(b_ranked, 1)

            pe.wait_ge(b_onehot, 1)
            turn_tiles(0, 0, 0, 0, True)
            pair_up(0, 0, True)
            paired(pe, UNITS, unit)
            prefix(1)

            def turn(mode):
                pe.wait_ge(k_chain, 8 * mode + 2)
                tail = scan_out[0][:, SJ - 1, :] if mode == 0 else got_rows[0][:, CJ - 1, :]
                nc.tensor.transpose(ps_turn[0:D, 0:P], whole_w[:, :], ident[:, :])
                nc.tensor.transpose(ps_turn[0:D, P:2 * P], tail, ident[:, :]).then_inc(k_turned, 1)
                pe.wait_ge(k_chain, 8 * mode + 7)
                nc.tensor.transpose(ps_turn[:, 2 * P:2 * P + D], carry_t[:, 0:P], ident[0:D, 0:D]
                                    ).then_inc(k_back, 1)

            def node_step(mode):
                F, wa, wb = (D, v1_s, v2_s) if mode else (3 * A, w1_s, w2_s)

                def step(g, h, i):
                    k = g + (mode * STEPS + 1)
                    pe.wait_ge(m_cat, k)
                    for t in range(SW):
                        mm = nc.tensor.transpose(ps_cat[0:3 * A, t * P:(t + 1) * P], cat[h][:, t, :], ident[:, :])
                    mm.then_inc(m_turned, 1)
                    pe.wait_ge(m_copied, k)
                    for e in range(2):
                        mm = nc.tensor.matmul(ps_hid[e], wa[:, :], cat_t[0:F, e * HALF:(e + 1) * HALF],
                                              start=True, stop=True)
                    mm.then_inc(m_hid, 1)
                    pe.wait_ge(m_relu, k)
                    if mode or not (isinstance(g, int) and g == 0):
                        pe.wait_ge(m_done, g + mode * STEPS)
                    for t in range(SW):
                        mm = nc.tensor.matmul(ps_node[:, t * D:(t + 1) * D], hid[:, t * P:(t + 1) * P],
                                              wb[:, :], start=True, stop=True)
                    mm.then_inc(m_node, 1)
                paired(pe, STEPS, step)

            pe.wait_ge(s_w, WLOAD)
            for mode in range(3):
                turn(mode)
                if mode < 2:
                    node_step(mode)

        @block.vector
        def _(dve):
            V = nc.vector
            V.memset(xs[:, W - 1, :], 0.0)
            V.memset(dst_side[:, :], -1).then_inc(s_xpad, 1)
            V.memset(ones[:, :], 1.0)
            V.memset(keys[:, :, COLS:KP], 0.0)
            V.memset(zeros_b[:, :], 0.0)
            V.memset(nothing[0][:, :, 0:A], 0.0)
            V.memset(nothing[0][:, :, A:D], -BIG)
            V.memset(nothing[1][:, :, :], 0.0)
            V.memset(carry_t[:, 0:1], 0.0)
            V.memset(sentinel[:, :], -1.0).then_inc(s_keep, 1)
            dve.wait_ge(s_iota, 2)
            for t in (ident, ident_b):
                V.tensor_scalar(t[:, :], diff[:, :], 0.0, None, ALU.is_equal)
            for t in (before, before_b):
                V.tensor_scalar(t[:, :], diff[:, :], 0.0, None, ALU.is_gt)
            V.tensor_copy(col[:, :, :].rearrange("p w t -> p (w t)"), col_i).then_inc(s_const, 1)
            dve.wait_ge(s_const, 1)
            dve.wait_ge(s_src, 16)
            V.tensor_scalar(part[0], src_i[:, :], P - 1, None, ALU.bitwise_and).then_inc(s_part, 1)
            V.tensor_scalar(part[1], src_i[:, :], 7, None, ALU.logical_shift_right).then_inc(s_part, 1)
            dve.wait_ge(s_dst, 48)
            V.tensor_scalar(part[2], dst_i, P - 1, None, ALU.bitwise_and).then_inc(s_part, 1)
            V.tensor_scalar(part[3], dst_i, 7, None, ALU.logical_shift_right).then_inc(s_part, 1)
            V.tensor_copy(edge_key[1][:, 0:1], dst_i[:, 0:1])
            V.tensor_copy(edge_key[1][:, 1:2], dst_i[:, COLS - 1:COLS])
            V.tensor_copy(edge_key[1][:, 2:3], dst_side[:, 1:2])
            V.tensor_tensor(cont[:, 0:1], dst_i[:, 0:1], dst_side[:, 0:1], ALU.is_equal)
            V.tensor_tensor(cont[:, 1:COLS], dst_i[:, 1:COLS], dst_i[:, 0:COLS - 1],
                            ALU.is_equal).then_inc(s_const, 1)
            dve.wait_ge(s_keys, 4)

            def onehots(v, b, outs):
                for k, o, n in outs:
                    op = V.tensor_tensor(o[b][:, :, :], col[:, 0:n, :],
                                         keys[:, k, bass.ds(v * UT, UT)].unsqueeze(1).to_broadcast([P, n, UT]),
                                         ALU.is_equal)
                return op

            def count(v, b, i):
                if not at_start(v):
                    dve.wait_ge(a_used, v - 1)
                onehots(v, b, ((0, lo, P), (1, hi, W))).then_inc(a_onehot, 1)

            paired(dve, UNITS, count)

            chain = [0]

            def link(op):
                chain[0] += 1
                op.then_inc(n_chain, 1)
                dve.wait_ge(n_chain, chain[0])

            def prefix(k, counts):
                V.tensor_copy(cnt[k][:, :], counts).then_inc(n_cnt, 1)
                dve.wait_ge(n_cnt, k + 1)
                dve.wait_ge(n_sums, k + 1)
                link(V.tensor_copy(total[:, :], ps_small[1]))
                link(V.tensor_tensor_scan(incl[:, :], ones[:, 0:W], total[:, :], 0.0, ALU.mult, ALU.add))
                link(V.tensor_tensor(incl[:, :], incl[:, :], total[:, :], ALU.subtract))
                link(V.tensor_tensor(base[:, :], incl[:, :], ps_small[0], ALU.add))
                link(V.tensor_scalar(has[:, :], cnt[k][:, :], 0.0, None, ALU.is_gt))
                link(V.tensor_tensor(last[:, :], base[:, :], cnt[k][:, :], ALU.add))
                link(V.scalar_tensor_tensor(last[:, :], last[:, :], float(-1 - E), has[:, :], ALU.add, ALU.mult))
                link(V.tensor_scalar(end_row[k][:, :], last[:, :], float(E), None, ALU.add))

            dve.wait_ge(a_used, UNITS)
            prefix(0, ps_src)
            V.tensor_scalar(base[:, :], base[:, :], 1.0, None, ALU.add).then_inc(n_seed, 1)
            link(V.tensor_scalar(inv_cnt[:, :], cnt[0][:, :], 1.0, None, ALU.max))
            link(V.reciprocal(inv_cnt[:, :], inv_cnt[:, :]))

            def rank_onehots(v, b):
                if not at_start(v):
                    dve.wait_ge(b_picked, v * 2 - 2)
                onehots(v, b, ((0, lo, P), (1, hi, W), (2, dlo, P), (3, dhi, W))).then_inc(b_onehot, 1)

            def place(b, g, h):
                dve.wait_ge(b_same, g + 1)
                V.tensor_tensor(same[h][:, :, :], ps_same.rearrange("p (t e) -> p t e", e=P),
                                before_b[:, :].unsqueeze(1).to_broadcast([P, GT, P]),
                                ALU.mult).then_inc(b_masked, 1)
                dve.wait_ge(b_ranked, g + 1)
                V.tensor_tensor(picked[:, :, :], ps_rank[h].rearrange("p (t w) -> p t w", w=W),
                                hi[b][:, :, h * GT:(h + 1) * GT].rearrange("p w t -> p t w"),
                                ALU.mult).then_inc(b_picked, 1)
                dve.wait_ge(b_picked, g + 1)
                dve.wait_ge(b_rows, g + 1)
                V.tensor_reduce(rank[b][h][:, :], picked[:, :, :], AX, ALU.add).then_inc(b_pos, 1)

            def unit(v, b, i):
                if not at_end(v, UNITS):
                    rank_onehots(v + 1, 1 - b)
                place(b, v * 2, 0)
                if not at_end(v, UNITS):
                    place(b, v * 2 + 1, 1)

            rank_onehots(0, 0)
            paired(dve, UNITS, unit)

            dve.wait_ge(b_ranked, GROUPS)
            prefix(1, ps_dst)
            V.tensor_scalar(last[:, :], cnt[1][:, :], 1.0, None, ALU.add).then_inc(n_deg, 1)
            dve.wait_ge(n_root, 1)
            link(V.reciprocal(dis[:, :], root[:, :]))
            dve.wait_ge(s_x, 32)
            dve.wait_ge(s_w, WLOAD)
            link(V.tensor_tensor(xs[:, :, :], xs[:, :, :], b2_s[:, :].unsqueeze(1).to_broadcast([P, W, D]),
                                 ALU.add))
            link(V.scalar_tensor_tensor(bias0[:, :], bcol[:, 1:2], bcol[:, 2:3], bcol[:, 0:1],
                                        ALU.mult, ALU.add))

            def scan(g, h, i):
                dve.wait_ge(c_in[h], i * 32 + 32)
                if not (isinstance(g, int) and g == 0):
                    dve.wait_ge(c_scan, g)
                e = scan_in[h].rearrange("p (j f) -> p j f", f=ROW)
                V.tensor_tensor(flag[:, :], e[:, 1:SJ + 1, A], e[:, 0:SJ, A], ALU.is_equal).then_inc(c_flag, 1)
                dve.wait_ge(c_flag, g * 3 + 1)
                V.tensor_reduce(whole_c[:, bass.ds(g, 1)], flag[:, :], AX, ALU.min)
                V.tensor_scalar(sign[:, :], flag[:, :], 2.0, -1.0, ALU.mult, ALU.add).then_inc(c_flag, 1)
                if isinstance(g, int) and g == 0:
                    V.tensor_copy(first_cont[0][:, :], flag[:, 0:1])
                    V.tensor_copy(edge_key[0][:, 0:1], e[:, 1, A:A + 1])
                if at_end(g, SCHUNKS):
                    V.tensor_copy(edge_key[0][:, 1:2], e[:, SJ, A:A + 1])
                dve.wait_ge(c_flag, g * 3 + 2)
                V.tensor_scalar(limit[:, :], sign[:, :], BIG, None, ALU.mult).then_inc(c_flag, 1)
                dve.wait_ge(c_flag, g * 3 + 3)
                if not at_start(g):
                    dve.wait_ge(c_out[h], i * 16)
                for f in range(A):
                    for at, ctl, op0, op1, none in ((f, flag, ALU.mult, ALU.add, 0.0),
                                                    (A + f, limit, ALU.min, ALU.max, -BIG)):
                        before_it = none if isinstance(g, int) and g == 0 else scan_out[1 - h][:, SJ - 1, at:at + 1]
                        op = V.tensor_tensor_scan(scan_out[h][:, :, at], ctl[:, :], e[:, 1:SJ + 1, f],
                                                  before_it, op0, op1)
                op.then_inc(c_scan, 1)

            paired(dve, SCHUNKS, scan)

            def carries(mode):
                base_k, step = 8 * mode, [0]
                k = min(mode, 1)

                def klink(op):
                    step[0] += 1
                    op.then_inc(k_chain, 1)
                    dve.wait_ge(k_chain, base_k + step[0])

                if mode == 0:
                    dve.wait_ge(c_scan, SCHUNKS)
                    klink(V.tensor_reduce(whole[0][:, :], whole_c[:, :], AX, ALU.min))
                    dve.wait_ge(c_next, 16)
                else:
                    dve.wait_ge(g_chain, mode * LINKS)
                    klink(V.tensor_reduce(whole[1][:, :], cont[:, :], AX, ALU.min))
                klink(V.tensor_copy(whole_w[:, :], whole[k][:, 0:1].to_broadcast([P, D])))
                dve.wait_ge(k_turned, mode + 1)
                klink(V.tensor_copy(turned[:, :], ps_turn[0:D, 0:2 * P]))
                klink(V.tensor_scalar(sign_t[:, :], turned[:, 0:P], 2.0, -1.0, ALU.mult, ALU.add))
                klink(V.tensor_scalar(limit_t[:, :], sign_t[:, :], BIG, None, ALU.mult))
                S = A if mode == 0 else D
                klink(V.tensor_tensor_scan(carry_t[0:S, 1:P + 1], turned[0:S, 0:P], turned[0:S, P:2 * P],
                                           0.0, ALU.mult, ALU.add))
                if mode == 0:
                    klink(V.tensor_tensor_scan(carry_t[A:D, 1:P + 1], limit_t[A:D, :], turned[A:D, P:2 * P],
                                               -BIG, ALU.min, ALU.max))
                else:
                    klink(V.memset(carry_t[:, 0:1], 0.0))
                f0 = first_cont[0][:, :] if mode == 0 else cont[:, 0:1]
                key = edge_key[k]
                if mode < 2:
                    link(V.tensor_tensor(work[:, 0:1], key[:, 1:2], key[:, 2:3], ALU.is_equal))
                    link(V.tensor_tensor(work[:, 1:2], work[:, 0:1], whole[k][:, :], ALU.mult))
                    link(V.tensor_scalar(work[:, 2:3], work[:, 1:2], -1.0, 1.0, ALU.mult, ALU.add))
                    link(V.tensor_tensor(work[:, 0:1], work[:, 2:3], f0, ALU.mult))
                    link(V.scalar_tensor_tensor(work[:, 1:2], key[:, 0:1], float(-NPAD), work[:, 0:1],
                                                ALU.add, ALU.mult))
                    link(V.tensor_scalar(target[k][:, :], work[:, 1:2], float(NPAD), None, ALU.add))
                dve.wait_ge(k_back, mode + 1)
                klink(V.tensor_copy(carry[:, :], ps_turn[:, 2 * P:2 * P + D]))


            def node_stage(mode):
                def window(t, g):
                    return t[:, bass.ds(g * SW, SW), :]

                def wide(t, g, n):
                    return t[:, bass.ds(g * SW, SW)].unsqueeze(2).to_broadcast([P, SW, n])

                def features(g, h, i):
                    step = [0]

                    def mlink(op):
                        step[0] += 1
                        op.then_inc(m_link, 1)
                        dve.wait_ge(m_link, g * 2 + (2 * mode * STEPS + step[0]))

                    for k in range(SW):
                        dve.wait_ge(m_got[h][k], i * 16 + 16 * (mode * STEPS // 2 + 1))
                    dve.wait_ge(m_corr[h], i * 16 + 16 * (mode * STEPS // 2 + 1))
                    c = cat[h]
                    if mode == 0:
                        mlink(V.tensor_tensor(c[:, :, 0:A], window(agg, g)[:, :, 0:A], corr[h][:, :, 0:A], ALU.add))
                        mlink(V.tensor_tensor(c[:, :, A:D], window(agg, g)[:, :, A:D], corr[h][:, :, A:D], ALU.max))
                        V.tensor_tensor(c[:, :, D:3 * A], c[:, :, 0:A], wide(inv_cnt, g, A),
                                        ALU.mult).then_inc(m_cat, 1)
                    else:
                        dve.wait_ge(m_cat, g + mode * STEPS)
                        mlink(V.tensor_tensor(sq[:, :, :], window(agg, g), corr[h][:, :, :], ALU.add))
                        mlink(V.tensor_tensor(sq[:, :, :], sq[:, :, :], window(ys, g), ALU.add))
                        V.tensor_tensor(c[:, :, 0:D], sq[:, :, :], wide(dis, g, D), ALU.mult).then_inc(m_cat, 1)

                def result(g, h, i):
                    if mode == 1:
                        dve.wait_ge(m_node, g + (STEPS + 1))
                        V.tensor_tensor(window(ys, g), ps_node.rearrange("p (t f) -> p t f", f=D),
                                        wide(dis, g, D), ALU.mult).then_inc(m_done, 1)
                        return
                    step = [0]
                    first = 0 if mode == 0 else 7 * STEPS

                    def clink(op):
                        step[0] += 1
                        op.then_inc(m_chain, 1)
                        dve.wait_ge(m_chain, g * 7 + (first + step[0]))

                    def spread(k):
                        return stat[:, k, :].unsqueeze(2).to_broadcast([P, SW, D])

                    if mode == 0:
                        dve.wait_ge(m_node, g + 1)
                        clink(V.tensor_tensor(mid[:, :, :], ps_node.rearrange("p (t f) -> p t f", f=D),
                                              window(xs, g), ALU.add))
                    else:
                        dve.wait_ge(m_cat, g + (2 * STEPS + 1))
                        dve.wait_ge(m_done, g + 2 * STEPS)
                        clink(V.tensor_tensor(mid[:, :, :], cat[h][:, :, 0:D], window(xs, g), ALU.add))
                    clink(V.tensor_reduce(stat[:, 0, :], mid[:, :, :], AX, ALU.add))
                    clink(V.tensor_scalar(stat[:, 0, :], stat[:, 0, :], -1.0 / D, None, ALU.mult))
                    clink(V.tensor_tensor(mid[:, :, :], mid[:, :, :], spread(0), ALU.add))
                    clink(V.tensor_tensor(sq[:, :, :], mid[:, :, :], mid[:, :, :], ALU.mult))
                    clink(V.tensor_reduce(stat[:, 0, :], sq[:, :, :], AX, ALU.add))
                    V.tensor_scalar(stat[:, 1, :], stat[:, 0, :], 1.0 / D, EPS, ALU.mult, ALU.add).then_inc(m_var, 1)
                    dve.wait_ge(m_root, g + (mode // 2 * STEPS + 1))
                    clink(V.reciprocal(stat[:, 3, :], stat[:, 2, :]))
                    if mode == 0:
                        V.tensor_tensor(res[0][:, :, :], mid[:, :, :], spread(3), ALU.mult).then_inc(s_xready, 1)
                        dve.wait_ge(s_xready, g + 1)
                        V.tensor_tensor(window(xs, g), res[0][:, :, :],
                                        c2_s[:, :].unsqueeze(1).to_broadcast([P, SW, D]), ALU.add)
                        V.tensor_tensor(window(ys, g), res[0][:, :, :], wide(dis, g, D),
                                        ALU.mult).then_inc(m_done, 1)
                    else:
                        if not at_start(g):
                            dve.wait_ge(m_store[h], i * 16 + 16 * STEPS)
                        V.tensor_tensor(res[h][:, :, :], mid[:, :, :], spread(3), ALU.mult).then_inc(m_done, 1)

                features(0, 0, 0)

                def body(g, h, i):
                    features(g + 1, 1 - h, i + h)
                    result(g, h, i)
                paired(dve, STEPS - 1, body)
                result(STEPS - 1, 1, STEPS // 2 - 1)

            carries(0)
            node_stage(0)
            for q in range(2):
                def add_up(g, h, i):
                    if not at_start(g):
                        dve.wait_ge(g_chain, g * CJ + (q * LINKS - CJ - 1))
                    V.tensor_copy(gflag[h][:, :], cont[:, bass.ds(g * CJ, CJ)]).then_inc(g_flag, 1)
                    dve.wait_ge(g_flag, g + (q * CHUNKS + 1))
                    for j in range(CJ):
                        dve.wait_ge(g_got[h][j], i * 16 + (16 * q * G_HALF[h] + 16))
                        if isinstance(g, int) and g == 0 and j == 0:
                            continue
                        if not (isinstance(g, int) and g == 0 and j == 1 and q == 0):
                            dve.wait_ge(g_chain, g * CJ + (q * LINKS + j - 1))
                        prior = got_rows[h][:, j - 1, :] if j else got_rows[1 - h][:, CJ - 1, :]
                        V.scalar_tensor_tensor(got_rows[h][:, j, :], prior, gflag[h][:, j:j + 1],
                                               got_rows[h][:, j, :], ALU.mult, ALU.add).then_inc(g_chain, 1)
                paired(dve, CHUNKS, add_up)
                carries(q + 1)
                node_stage(q + 1)


_INS = ["x", "src", "dst", "edge_attr_32", "L0_gnn_u", "L0_gnn_W1", "L0_gnn_b1", "L0_gnn_W2", "L0_gnn_b2",
        "L1_gnn_W1", "L1_gnn_b1", "L1_gnn_W2", "L1_gnn_b2"]


def kernel(**inputs):
    import numpy as np
    import concourse.bacc as bacc
    from concourse.bass_utils import run_bass_kernel_spmd as run

    nc = bacc.Bacc("TRN2", target_bir_lowering=False, num_devices=1)
    arrays, args = {}, []
    for name in _INS:
        a = np.ascontiguousarray(inputs[name])
        arrays[f"in_{name}"] = a
        args.append(nc.dram_tensor(f"in_{name}", a.shape, mybir.dt.from_np(a.dtype), kind="ExternalInput").ap())
    result = nc.dram_tensor("result", (N, D), F32, kind="ExternalOutput").ap()
    build(nc, *args, result)
    r = run(nc, [arrays], core_ids=[0])
    return r.results[0]["result"]
```

```python
from contextlib import ExitStack

import concourse.bass as bass
from concourse import mybir

F32, BF16, I32 = mybir.dt.float32, mybir.dt.bfloat16, mybir.dt.int32
ALU = mybir.AluOpType
ACT = mybir.ActivationFunctionType
AX = mybir.AxisListType.X

P = 128
N, E = 12500, 400000
COLS = E // P
W = -(-N // P)
NPAD = W * P
LASTROWS = N - (W - 1) * P
D, A, HID = 64, 32, 128
ROW = A + 1
GT = 5
GROUPS = COLS // GT
UT = 2 * GT
UNITS = -(-COLS // UT)
DEEP = 2
SJ = 125
SCHUNKS = COLS // SJ
CJ = 25
CHUNKS = COLS // CJ
SW = 7
STEPS = W // SW
BIG = 3.4e38
EPS = 1e-5
assert E % P == 0 and GROUPS * GT == COLS and GROUPS % 2 and UNITS % 2 and SCHUNKS % 2 and CHUNKS % 2 and STEPS * SW == W


def rounds(eng, count, n, body):
    for k in range(n):
        body(k, k, 0)
    with eng.Fori(1, count // n) as i:
        for k in range(n):
            body(i * n + k, k, i)
    for k in range(count % n):
        body(count // n * n + k, k, count // n)


def paired(eng, count, body):
    rounds(eng, count, 2, body)


def build(nc, x, src, dst, attr, u, w1, b1, w2, b2, v1, c1, v2, c2, out):
    with ExitStack() as ctx:
        def sb(name, shape, dt=F32):
            return ctx.enter_context(nc.sbuf_tensor(name, shape, dt))

        def pair(name, shape, dt=F32):
            return [sb(f"{name}{h}", shape, dt) for h in range(2)]

        def sem(name):
            return ctx.enter_context(nc.semaphore(name))

        def dram(name, shape):
            return nc.dram_tensor(name, shape, F32, kind="Internal").ap()

        by_src = dram("by_src", (E + 2, ROW))
        running = [dram(f"running{k}", (E + 1, D)) for k in range(3)]
        correction = [dram(f"correction{k}", (NPAD, D)) for k in range(3)]
        table = [dram(f"table{k}", (NPAD, D)) for k in range(2)]

        def node_view(t):
            return t.rearrange("(w l) f -> l w f", l=P)

        def edge_view(t, first=0):
            return t[first:first + E, :].rearrange("(p j) f -> p (j f)", p=P)

        ps = ctx.enter_context(nc.psum_tensor("ps", [P, 8 * 512], F32))
        ps_src = ps[:, 0:W]
        ps_dst = ps[:, 512:512 + W]
        ps_small = [ps[:, 1024:1024 + W], ps[:, 1024 + P:1024 + P + W]]
        ps_lot = ps[:, 1024:1024 + GT * P // 2].bitcast(BF16)
        ps_same = ps[:, 1536:1536 + GT * P]
        ps_rank = [ps[:, 2560 + 512 * h:2560 + 512 * h + GT * W] for h in range(2)]
        HALF = SW * P // 2
        ps_cat = ps[:, 1536:1536 + SW * P]
        ps_hid = [ps[:, 2560 + 512 * h:2560 + 512 * h + HALF] for h in range(2)]
        ps_node = ps[:, 3584:3584 + SW * D]
        ps_turn = ps[:, 0:512]

        diff = sb("diff", [P, P], I32)
        col = sb("col", [P, P, UT], BF16)
        ident = sb("ident", [P, P])
        ident_b = sb("ident_b", [P, P], BF16)
        before = sb("before", [P, P])
        before_b = sb("before_b", [P, P], BF16)
        ones = sb("ones", [P, P])
        zeros_b = sb("zeros_b", [P, P], BF16)
        nothing = pair("nothing", [P, SW, D])
        sentinel = sb("sentinel", [P, D])

        arena = sb("arena", [P, 2 * SJ * D])
        scan_out = [arena[:, h * SJ * D:(h + 1) * SJ * D].rearrange("p (j f) -> p j f", f=D) for h in range(2)]
        agg = arena[:, 0:W * D].rearrange("p (w f) -> p w f", f=D)
        ys = arena[:, SJ * D:SJ * D + W * D].rearrange("p (w f) -> p w f", f=D)
        dst_i = arena[:, 0:COLS].bitcast(I32)
        part = [arena[:, (k + 1) * COLS:(k + 2) * COLS].bitcast(I32) for k in range(4)]
        INLEN = (SJ + 1) * ROW
        arena2 = sb("arena2", [P, 2 * INLEN])
        KP = UNITS * UT
        keys = arena2[:, 0:2 * KP].bitcast(BF16).rearrange("p (k j) -> p k j", k=4)
        col_i = arena2[:, 2 * KP:2 * KP + P * UT].bitcast(I32)
        scan_in = [arena2[:, h * INLEN:(h + 1) * INLEN] for h in range(2)]
        got_rows = [arena2[:, h * CJ * D:(h + 1) * CJ * D].rearrange("p (j f) -> p j f", f=D) for h in range(2)]

        src_i = sb("src_i", [P, COLS], I32)
        cont = sb("cont", [P, COLS])

        lo = pair("lo", [P, P, UT], BF16)
        hi = pair("hi", [P, W, UT], BF16)
        dlo = pair("dlo", [P, P, UT], BF16)
        dhi = pair("dhi", [P, W, UT], BF16)
        lot_b = pair("lot_b", [P, GT * P], BF16)
        lot_f = pair("lot_f", [P, GT * P])
        same = pair("same", [P, GT, P], BF16)
        snap = pair("snap", [P, W])
        picked = sb("picked", [P, GT, W])
        rank = [pair(f"rank{b}", [P, GT], I32) for b in range(DEEP)]
        attr_in = pair("attr_in", [P, GT, A])
        rows = [pair(f"rows{b}", [P, GT, ROW]) for b in range(DEEP)]

        flag = sb("flag", [P, SJ])
        sign = sb("sign", [P, SJ])
        limit = sb("limit", [P, SJ])
        whole_c = sb("whole_c", [P, SCHUNKS])
        gflag = pair("gflag", [P, CJ])
        gidx = pair("gidx", [P, CJ], I32)

        cnt = pair("cnt", [P, W])
        total = sb("total", [P, W])
        incl = sb("incl", [P, W])
        base = sb("base", [P, W])
        has = sb("has", [P, W])
        last = sb("last", [P, W])
        end_row = pair("end_row", [P, W], I32)
        inv_cnt = sb("inv_cnt", [P, W])
        root = sb("root", [P, W])
        dis = sb("dis", [P, W])
        xs = sb("xs", [P, W, D])
        corr = pair("corr", [P, SW, D])
        NODE = 2 * CJ * D
        cat_t = arena2[0:3 * A, NODE:NODE + SW * P]
        hid = arena2[:, NODE + SW * P:NODE + 2 * SW * P]
        mid, sq, *res = (arena2[:, NODE + 2 * SW * P + k * SW * D:NODE + 2 * SW * P + (k + 1) * SW * D]
                         .rearrange("p (w f) -> p w f", f=D) for k in range(4))
        stat = sb("stat", [P, 4, SW])

        CAT = NODE + 2 * SW * P + 4 * SW * D
        cat = [arena2[:, CAT + h * SW * 3 * A:CAT + (h + 1) * SW * 3 * A].rearrange("p (w f) -> p w f", f=3 * A)
               for h in range(2)]

        whole = pair("whole", [P, 1])
        edge_key = [sb(f"edge_key{k}", [P, 3]) for k in range(2)]
        first_cont = pair("first_cont", [P, 1])
        dst_side = sb("dst_side", [P, 2], I32)
        work = sb("work", [P, 4])
        target = pair("target", [P, 1], I32)
        whole_w = sb("whole_w", [P, D])
        turned = sb("turned", [D, 2 * P])
        sign_t = sb("sign_t", [D, P])
        limit_t = sb("limit_t", [D, P])
        carry_t = sb("carry_t", [D, P + 1])
        carry = sb("carry", [P, D])

        w1_s = sb("w1_s", [3 * A, HID])
        w2_s = sb("w2_s", [HID, D])
        v1_s = sb("v1_s", [D, HID])
        v2_s = sb("v2_s", [HID, D])
        bcol = sb("bcol", [P, 4])
        bias0 = sb("bias0", [P, 1])
        b2_s = sb("b2_s", [P, D])
        c2_s = sb("c2_s", [P, D])

        s_src, s_dst, s_x, s_w, s_iota, s_const, s_init, s_keep = (sem(n) for n in (
            "s_src", "s_dst", "s_x", "s_w", "s_iota", "s_const", "s_init", "s_keep"))
        s_part, s_keys, s_xready, s_xpad, s_xb = (sem(n) for n in ("s_part", "s_keys", "s_xready", "s_xpad", "s_xb"))
        a_onehot, a_used = (sem(n) for n in ("a_onehot", "a_used"))
        n_cnt, n_sums, n_chain, n_seed, n_deg, n_root = (sem(n) for n in (
            "n_cnt", "n_sums", "n_chain", "n_seed", "n_deg", "n_root"))
        b_onehot, b_turned, b_copied, b_same, b_masked = (sem(n) for n in (
            "b_onehot", "b_turned", "b_copied", "b_same", "b_masked"))
        b_snap, b_state, b_looked, b_ranked, b_picked, b_pos, b_rows, b_seen = (sem(n) for n in (
            "b_snap", "b_state", "b_looked", "b_ranked", "b_picked", "b_pos", "b_rows", "b_seen"))
        b_attr = [sem(f"b_attr{h}") for h in range(2)]
        row_dma = [sem(f"row_dma{k}") for k in range(2 * CJ)]
        b_scat = [[row_dma[(2 * b + h) * GT:][:GT] for h in range(2)] for b in range(DEEP)]
        g_got = [row_dma[h * CJ:][:CJ] for h in range(2)]
        scattered = [16 * len(range(k // GT, GROUPS, 2 * DEEP)) if k < 2 * DEEP * GT else 0
                     for k in range(2 * CJ)]
        c_in = [sem(f"c_in{h}") for h in range(2)]
        c_out = [sem(f"c_out{h}") for h in range(2)]
        c_next, c_flag, c_scan = sem("c_next"), sem("c_flag"), sem("c_scan")
        g_staged, g_seen, g_flag, g_chain = (sem(n) for n in (
            "g_staged", "g_seen", "g_flag", "g_chain"))
        g_out = [sem(f"g_out{h}") for h in range(2)]
        k_chain, k_turned, k_back, k_scat = (sem(n) for n in (
            "k_chain", "k_turned", "k_back", "k_scat"))
        m_got = [[sem(f"m_got{h}_{k}") for k in range(SW)] for h in range(2)]
        m_corr = [sem(f"m_corr{h}") for h in range(2)]
        m_link, m_cat, m_turned, m_copied, m_hid, m_relu, m_node, m_chain, m_var, m_root, m_done = (
            sem(n) for n in ("m_link", "m_cat", "m_turned", "m_copied", "m_hid", "m_relu", "m_node",
                             "m_chain", "m_var", "m_root", "m_done"))
        m_store = [sem(f"m_store{h}") for h in range(2)]
        ctx.enter_context(nc.allow_non_contiguous_dma(reason="columns of 128 numbers"))
        ctx.enter_context(nc.allow_low_precision(reason="a sum with one term that isn't zero, a whole number"))
        block = ctx.enter_context(nc.Block())

        G_HALF = [CHUNKS - CHUNKS // 2, CHUNKS // 2]
        C_HALF = [SCHUNKS - SCHUNKS // 2, SCHUNKS // 2]
        LINKS = COLS - 1
        INIT = 16 * (3 * STEPS + 3 + 2)
        WLOAD = 16 * 10

        def at_end(g, count):
            return isinstance(g, int) and g == count - 1

        def at_start(g):
            return isinstance(g, int) and g < 2

        @block.sync
        def _(sp):
            sp.dma_start(src_i[:, :], src.rearrange("(p j) -> p j", p=P)).then_inc(s_src, 16)
            sp.dma_start(dst_i, dst.rearrange("(p j) -> p j", p=P)).then_inc(s_dst, 16)
            sp.wait_ge(s_xpad, 1)
            dst_rows = dst.rearrange("(p j a) -> p j a", p=P, a=1)
            sp.dma_start(dst_side[1:P, 0:1], dst_rows[0:P - 1, COLS - 1, :]).then_inc(s_dst, 16)
            sp.dma_start(dst_side[0:P - 1, 1:2], dst_rows[1:P, 0, :]).then_inc(s_dst, 16)
            sp.dma_start(xs[:, 0:W - 1, :],
                         x[0:(W - 1) * P, :].rearrange("(w l) f -> l w f", l=P)).then_inc(s_x, 16)
            sp.dma_start(xs[0:LASTROWS, W - 1, :], x[(W - 1) * P:N, :]).then_inc(s_x, 16)
            for to, frm in ((w1_s[:, :], w1[0:3 * A, :]), (w2_s[:, :], w2), (v1_s[:, :], v1), (v2_s[:, :], v2),
                            (bcol[:, 0:1], b1.rearrange("(p a) -> p a", a=1)),
                            (bcol[:, 1:2], w1[3 * A:3 * A + 1, :].rearrange("a p -> p a")),
                            (bcol[:, 2:3], u[0:1, 0:1].to_broadcast([P, 1])),
                            (bcol[:, 3:4], c1.rearrange("(p a) -> p a", a=1)),
                            (b2_s[:, :], b2.rearrange("(a f) -> a f", a=1).to_broadcast([P, D])),
                            (c2_s[:, :], c2.rearrange("(a f) -> a f", a=1).to_broadcast([P, D]))):
                sp.dma_start(to, frm).then_inc(s_w, 16)
            sp.wait_ge(s_keep, 1)
            for k in range(3):
                sp.dma_start(running[k][E:E + 1, :], nothing[1][0:1, 0, :]).then_inc(s_init, 16)
            sp.dma_start(by_src[0:1, :], sentinel[0:1, 0:ROW]).then_inc(s_init, 16)
            sp.dma_start(by_src[E + 1:E + 2, :], sentinel[0:1, 0:ROW]).then_inc(s_init, 16)
            with sp.Fori(0, STEPS) as s:
                for k in range(3):
                    sp.dma_start(node_view(correction[k])[:, bass.ds(s * SW, SW), :],
                                 nothing[min(k, 1)][:, :, :]).then_inc(s_init, 16)

            def attributes(g, h, i):
                if not at_start(g):
                    sp.wait_ge(b_rows, g - 1)
                sp.dma_start(attr_in[h].rearrange("p t a -> p (t a)"),
                             edge_view(attr)[:, bass.ds(g * (GT * A), GT * A)]).then_inc(b_attr[h], 16)

            paired(sp, GROUPS, attributes)

            for b in range(DEEP):
                for h in range(2):
                    for k in range(GT):
                        sp.wait_ge(b_scat[b][h][k], scattered[(2 * b + h) * GT + k])
            sp.wait_ge(s_init, INIT)
            sp.dma_start(edge_key[0][:, 2:3], by_src[2:E + 2, :].rearrange("(p j) f -> p j f", p=P)[
                :, COLS - 1, A:A + 1]).then_inc(c_next, 16)

            def scan_load(g, h, i):
                if not at_start(g):
                    sp.wait_ge(c_scan, g - 1)
                sp.dma_start(scan_in[h][:, 0:ROW],
                             edge_view(by_src)[:, bass.ds(g * (SJ * ROW), ROW)]).then_inc(c_in[h], 16)
                sp.dma_start(scan_in[h][:, ROW:INLEN],
                             edge_view(by_src, 1)[:, bass.ds(g * (SJ * ROW), SJ * ROW)]).then_inc(c_in[h], 16)

            paired(sp, SCHUNKS, scan_load)

            def step_load(mode):
                def load(g, h, i):
                    if mode or not at_start(g):
                        sp.wait_ge(m_cat, mode * STEPS + g - 1)
                    sp.dma_start(corr[h][:, :, :],
                                 node_view(correction[mode])[:, bass.ds(g * SW, SW), :]).then_inc(m_corr[h], 16)
                return load

            def step_store(mode):
                def store(g, h, i):
                    sp.wait_ge(m_done, mode * STEPS + g + 1)
                    if mode < 2:
                        sp.dma_start(node_view(table[mode])[:, bass.ds(g * SW, SW), :],
                                     ys[:, bass.ds(g * SW, SW), :]).then_inc(m_store[h], 16)
                    elif at_end(g, STEPS):
                        sp.dma_start(out[g * SW * P:(W - 1) * P, :].rearrange("(w l) f -> l w f", l=P),
                                     res[h][:, 0:SW - 1, :]).then_inc(m_store[h], 16)
                        sp.dma_start(out[(W - 1) * P:N, :], res[h][0:LASTROWS, SW - 1, :]).then_inc(m_store[h], 16)
                    else:
                        sp.dma_start(out[0:(W - 1) * P, :].rearrange("(w l) f -> l w f", l=P)[
                            :, bass.ds(g * SW, SW), :], res[h][:, :, :]).then_inc(m_store[h], 16)
                return store

            def node_io(mode):
                sp.wait_ge(k_scat, 16 * (mode + 1))
                load, store = step_load(mode), step_store(mode)
                load(0, 0, 0)
                load(1, 1, 0)

                def body(g, h, i):
                    load(g + 2, h, i)
                    store(g, h, i)
                paired(sp, STEPS - 2, body)
                store(STEPS - 2, 0, 0)
                store(STEPS - 1, 1, 0)

            node_io(0)
            for q in range(2):
                def rows_out(g, h, i):
                    sp.wait_ge(g_chain, g * CJ + (q * LINKS + CJ - 1))
                    sp.dma_start(edge_view(running[q + 1])[:, bass.ds(g * (CJ * D), CJ * D)],
                                 got_rows[h].rearrange("p j f -> p (j f)")).then_inc(g_out[h], 16)
                paired(sp, CHUNKS, rows_out)
                node_io(q + 1)
            for h in range(2):
                sp.wait_ge(m_store[h], 16 * (3 * STEPS // 2 + h))

        @block.gpsimd
        def _(pool):
            nc.gpsimd.iota(diff[:, :], [[1, P]], base=0, channel_multiplier=-1).then_inc(s_iota, 1)
            nc.gpsimd.iota(col_i, [[1, P], [0, UT]], base=0, channel_multiplier=0).then_inc(s_iota, 1)

            def scatter(v, b, i):
                for h in range(1 if at_end(v, UNITS) else 2):
                    pool.wait_ge(b_pos, v * 2 + (h + 1))
                    pool.sem_inc(b_seen, 1)
                    pool.wait_ge(b_rows, v * 2 + (h + 1))
                    pool.sem_inc(b_seen, 1)
                    for k in range(GT):
                        nc.gpsimd.indirect_dma_start(
                            out=by_src, out_offset=bass.IndirectOffsetOnAxis(ap=rank[b][h][:, k:k + 1], axis=0),
                            in_=rows[b][h][:, k, :], in_offset=None).then_inc(b_scat[b][h][k], 16)

            pool.wait_ge(s_x, 32)
            pool.wait_ge(s_w, WLOAD)
            nc.gpsimd.tensor_tensor(xs[:, :, :], xs[:, :, :], b2_s[:, :].unsqueeze(1).to_broadcast([P, W, D]),
                                    ALU.add).then_inc(s_xb, 1)
            pool.wait_ge(s_init, INIT)
            rounds(pool, UNITS, DEEP, scatter)

            def aggregate(mode):
                pool.wait_ge(k_chain, 8 * mode + 8)
                nc.gpsimd.indirect_dma_start(
                    out=correction[mode],
                    out_offset=bass.IndirectOffsetOnAxis(ap=target[min(mode, 1)][:, 0:1], axis=0),
                    in_=carry[:, :], in_offset=None, bounds_check=NPAD - 1,
                    oob_is_err=False).then_inc(k_scat, 16)
                for h in range(2):
                    if mode == 0:
                        pool.wait_ge(c_out[h], 16 * C_HALF[h])
                    else:
                        pool.wait_ge(g_out[h], 16 * mode * G_HALF[h])
                if mode == 0:
                    pool.wait_ge(n_deg, 1)
                for w in range(W):
                    h, k, turn = w // SW % 2, w % SW, mode * STEPS // 2 + w // (2 * SW)
                    if turn:
                        pool.wait_ge(m_got[h][k], 16 * turn)
                    nc.gpsimd.indirect_dma_start(
                        out=agg[:, w, :], out_offset=None, in_=running[mode],
                        in_offset=bass.IndirectOffsetOnAxis(ap=end_row[min(mode, 1)][:, w:w + 1], axis=0),
                    ).then_inc(m_got[h][k], 16)

            aggregate(0)
            for q in range(2):
                for h in range(2):
                    pool.wait_ge(m_store[h], 16 * (q + 1) * (STEPS // 2))

                def gather(g, h, i):
                    pool.wait_ge(g_staged, g + (q * CHUNKS + 1))
                    pool.sem_inc(g_seen, 1)
                    if not at_start(g):
                        pool.wait_ge(g_out[h], i * 16 + 16 * q * G_HALF[h])
                        pool.sem_inc(g_seen, 1)
                        pool.wait_ge(g_chain, g * CJ + (q * LINKS - CJ))
                        pool.sem_inc(g_seen, 1)
                    for k in range(CJ):
                        nc.gpsimd.indirect_dma_start(
                            out=got_rows[h][:, k, :], out_offset=None, in_=table[q],
                            in_offset=bass.IndirectOffsetOnAxis(ap=gidx[h][:, k:k + 1], axis=0),
                            ).then_inc(g_got[h][k], 16)

                paired(pool, CHUNKS, gather)
                aggregate(q + 1)

        @block.scalar
        def _(act):
            def to_keys(k):
                act.wait_ge(s_part, k + 1)
                nc.scalar.copy(keys[:, k, 0:COLS], part[k]).then_inc(s_keys, 1)

            to_keys(0)
            to_keys(1)
            to_keys(2)
            to_keys(3)

            def copy_turned(g, h):
                act.wait_ge(b_turned, g + 1)
                nc.scalar.copy(lot_b[h][:, :], ps_lot)
                nc.scalar.copy(lot_f[h][:, :], ps_lot).then_inc(b_copied, 1)

            def snapshot(g, h, t):
                act.wait_ge(b_state, g * GT + (t + 1))
                if not (isinstance(g, int) and g * GT + t < 2):
                    act.wait_ge(b_looked, g * GT + (t - 1))
                nc.scalar.copy(snap[(h * GT + t) % 2][:, :], ps_src).then_inc(b_snap, 1)

            def unit(v, b, i):
                for h in range(1 if at_end(v, UNITS) else 2):
                    g = v * 2 + h
                    for t in range(GT):
                        snapshot(g, h, t)
                        if t == 2:
                            act.wait_ge(b_attr[h], v * 16 + 16)
                            if not (isinstance(v, int) and v < DEEP):
                                for k in range(GT):
                                    act.wait_ge(b_scat[b][h][k], i * 16)
                            nc.scalar.copy(rows[b][h][:, :, 0:A], attr_in[h][:, :, :])
                            nc.scalar.copy(rows[b][h][:, :, A], src_i[:, bass.ds(g * GT, GT)]).then_inc(b_rows, 1)
                    if not at_end(v, UNITS):
                        copy_turned(g + 1, 1 - h)

            copy_turned(0, 0)
            rounds(act, UNITS, DEEP, unit)

            act.wait_ge(n_deg, 1)
            nc.scalar.activation(root[:, :], last[:, :], ACT.Sqrt).then_inc(n_root, 1)

            def scan_store(g, h, i):
                act.wait_ge(c_scan, g + 1)
                act.dma_start(edge_view(running[0])[:, bass.ds(g * (SJ * D), SJ * D)],
                              scan_out[h].rearrange("p j f -> p (j f)")).then_inc(c_out[h], 16)

            paired(act, SCHUNKS, scan_store)

            def node_step(mode):
                F = D if mode else 3 * A
                bias = bcol[:, 3:4] if mode else bias0[:, 0:1]

                def features(g):
                    act.wait_ge(m_turned, g + (mode * STEPS + 1))
                    nc.scalar.copy(cat_t[0:F], ps_cat[0:F, :]).then_inc(m_copied, 1)

                def hidden(g):
                    act.wait_ge(m_hid, g + (mode * STEPS + 1))
                    for e in range(2):
                        op = nc.scalar.activation(hid[:, e * HALF:(e + 1) * HALF], ps_hid[e], ACT.Relu, bias=bias)
                    op.then_inc(m_relu, 1)

                def deviation(g):
                    act.wait_ge(m_var, g + (mode // 2 * STEPS + 1))
                    nc.scalar.activation(stat[:, 2, :], stat[:, 1, :], ACT.Sqrt).then_inc(m_root, 1)

                def body(g, h, i):
                    if mode < 2:
                        features(g + 1)
                    if mode != 1:
                        deviation(g)
                    if mode < 2:
                        hidden(g + 1)

                if mode < 2:
                    features(0)
                    hidden(0)
                paired(act, STEPS - 1, body)
                if mode != 1:
                    deviation(STEPS - 1)

            node_step(0)
            for q in range(2):
                def stage_idx(g, h, i):
                    if q or not at_start(g):
                        act.wait_ge(g_chain, g * CJ + (q * LINKS - CJ - 1))
                    nc.scalar.copy(gidx[h][:, :], src_i[:, bass.ds(g * CJ, CJ)]).then_inc(g_staged, 1)
                paired(act, CHUNKS, stage_idx)
                node_step(q + 1)

        @block.tensor
        def _(pe):
            pe.wait_ge(s_const, 1)
            nc.tensor.matmul(ps_src, zeros_b[:, :], zeros_b[:, 0:W], start=True, stop=False,
                             skip_group_check=True)
            nc.tensor.matmul(ps_dst, zeros_b[:, :], zeros_b[:, 0:W], start=True, stop=False,
                             skip_group_check=True)

            def count(g, h, i):
                pe.wait_ge(a_onehot, g + 1)
                for t in range(UT if not at_end(g, UNITS) else COLS % UT):
                    mm = nc.tensor.matmul(ps_src, lo[h][:, :, t], hi[h][:, :, t], start=False, stop=False,
                                          skip_group_check=True)
                mm.then_inc(a_used, 1)

            paired(pe, UNITS, count)

            def prefix(k):
                pe.wait_ge(n_cnt, k + 1)
                nc.tensor.matmul(ps_small[0], before[:, :], cnt[k][:, :], start=True, stop=True)
                nc.tensor.matmul(ps_small[1], ones[:, :], cnt[k][:, :], start=True,
                                 stop=True).then_inc(n_sums, 1)

            prefix(0)
            pe.wait_ge(n_seed, 1)
            nc.tensor.matmul(ps_src, ident[:, :], base[:, :], start=True, stop=False,
                             skip_group_check=True).then_inc(b_state, 1)

            def turn_tiles(b, g, h):
                if not (isinstance(g, int) and g == 0):
                    pe.wait_ge(b_copied, g)
                for t in range(GT):
                    mm = nc.tensor.transpose(ps_lot[:, t * P:(t + 1) * P], lo[b][:, :, h * GT + t],
                                             ident_b[:, :])
                mm.then_inc(b_turned, 1)

            def pair_up(g, h):
                pe.wait_ge(b_copied, g + 1)
                for t in range(GT):
                    one = lot_b[h][:, t * P:(t + 1) * P]
                    mm = nc.tensor.matmul(ps_same[:, t * P:(t + 1) * P], one, one, start=True, stop=True)
                mm.then_inc(b_same, 1)

            def look_up(b, g, h, t):
                k = h * GT + t
                pe.wait_ge(b_snap, g * GT + (t + 1))
                nc.tensor.matmul(ps_src, lo[b][:, :, k], hi[b][:, :, k], start=False, stop=False,
                                 skip_group_check=True).then_inc(b_state, 1)
                mm = nc.tensor.matmul(ps_rank[h][:, t * W:(t + 1) * W], lot_f[h][:, t * P:(t + 1) * P],
                                      snap[k % 2][:, :], start=(t == 0), stop=False, skip_group_check=True)
                mm.then_inc(b_looked, 1)

            def unit(v, b, i):
                for h in range(1 if at_end(v, UNITS) else 2):
                    g = v * 2 + h
                    for t in range(GT):
                        if t == 2 and not at_end(v, UNITS):
                            if h == 1:
                                pe.wait_ge(b_onehot, v + 2)
                            turn_tiles(b if h == 0 else 1 - b, g + 1, 1 - h)
                        look_up(b, g, h, t)
                    for t in range(GT):
                        nc.tensor.matmul(ps_dst, dlo[b][:, :, h * GT + t], dhi[b][:, :, h * GT + t],
                                         start=False, stop=False, skip_group_check=True)
                    pe.wait_ge(b_masked, g + 1)
                    for t in range(GT):
                        mm = nc.tensor.matmul(ps_rank[h][:, t * W:(t + 1) * W], same[h][:, t, :],
                                              hi[b][:, :, h * GT + t], start=False, stop=(t == GT - 1),
                                              skip_group_check=True)
                    mm.then_inc(b_ranked, 1)
                    if not at_end(v, UNITS):
                        pair_up(g + 1, 1 - h)

            pe.wait_ge(b_onehot, 1)
            turn_tiles(0, 0, 0)
            pair_up(0, 0)
            paired(pe, UNITS, unit)
            prefix(1)

            def turn(mode):
                pe.wait_ge(k_chain, 8 * mode + 2)
                tail = scan_out[0][:, SJ - 1, :] if mode == 0 else got_rows[0][:, CJ - 1, :]
                nc.tensor.transpose(ps_turn[0:D, 0:P], whole_w[:, :], ident[:, :])
                nc.tensor.transpose(ps_turn[0:D, P:2 * P], tail, ident[:, :]).then_inc(k_turned, 1)
                pe.wait_ge(k_chain, 8 * mode + 7)
                nc.tensor.transpose(ps_turn[:, 2 * P:2 * P + D], carry_t[:, 0:P], ident[0:D, 0:D]
                                    ).then_inc(k_back, 1)

            def node_step(mode):
                F, wa, wb = (D, v1_s, v2_s) if mode else (3 * A, w1_s, w2_s)

                def turn_features(g, h):
                    pe.wait_ge(m_cat, g + (mode * STEPS + 1))
                    for t in range(SW):
                        mm = nc.tensor.transpose(ps_cat[0:3 * A, t * P:(t + 1) * P], cat[h][:, t, :], ident[:, :])
                    mm.then_inc(m_turned, 1)

                def hidden(g):
                    pe.wait_ge(m_copied, g + (mode * STEPS + 1))
                    for e in range(2):
                        mm = nc.tensor.matmul(ps_hid[e], wa[:, :], cat_t[0:F, e * HALF:(e + 1) * HALF],
                                              start=True, stop=True)
                    mm.then_inc(m_hid, 1)

                def outputs(g):
                    pe.wait_ge(m_relu, g + (mode * STEPS + 1))
                    if mode == 1:
                        pe.wait_ge(m_done, g + STEPS)
                    elif not (isinstance(g, int) and g == 0):
                        pe.wait_ge(m_chain, g * 7 - 6)
                    for t in range(SW):
                        mm = nc.tensor.matmul(ps_node[:, t * D:(t + 1) * D], hid[:, t * P:(t + 1) * P],
                                              wb[:, :], start=True, stop=True)
                    mm.then_inc(m_node, 1)

                def body(g, h, i):
                    turn_features(g + 1, 1 - h)
                    outputs(g)
                    hidden(g + 1)

                turn_features(0, 0)
                hidden(0)
                paired(pe, STEPS - 1, body)
                outputs(STEPS - 1)

            pe.wait_ge(s_w, WLOAD)
            for mode in range(3):
                turn(mode)
                if mode < 2:
                    node_step(mode)

        @block.vector
        def _(dve):
            V = nc.vector
            V.memset(xs[:, W - 1, :], 0.0)
            V.memset(dst_side[:, :], -1).then_inc(s_xpad, 1)
            V.memset(ones[:, :], 1.0)
            V.memset(keys[:, :, COLS:KP], 0.0)
            V.memset(zeros_b[:, :], 0.0)
            V.memset(nothing[0][:, :, 0:A], 0.0)
            V.memset(nothing[0][:, :, A:D], -BIG)
            V.memset(nothing[1][:, :, :], 0.0)
            V.memset(carry_t[:, 0:1], 0.0)
            V.memset(sentinel[:, :], -1.0).then_inc(s_keep, 1)
            dve.wait_ge(s_iota, 2)
            for t in (ident, ident_b):
                V.tensor_scalar(t[:, :], diff[:, :], 0.0, None, ALU.is_equal)
            for t in (before, before_b):
                V.tensor_scalar(t[:, :], diff[:, :], 0.0, None, ALU.is_gt)
            V.tensor_copy(col[:, :, :].rearrange("p w t -> p (w t)"), col_i).then_inc(s_const, 1)
            dve.wait_ge(s_const, 1)
            dve.wait_ge(s_src, 16)
            V.tensor_scalar(part[0], src_i[:, :], P - 1, None, ALU.bitwise_and).then_inc(s_part, 1)
            V.tensor_scalar(part[1], src_i[:, :], 7, None, ALU.logical_shift_right).then_inc(s_part, 1)
            dve.wait_ge(s_dst, 48)
            V.tensor_scalar(part[2], dst_i, P - 1, None, ALU.bitwise_and).then_inc(s_part, 1)
            V.tensor_scalar(part[3], dst_i, 7, None, ALU.logical_shift_right).then_inc(s_part, 1)
            V.tensor_copy(edge_key[1][:, 0:1], dst_i[:, 0:1])
            V.tensor_copy(edge_key[1][:, 1:2], dst_i[:, COLS - 1:COLS])
            V.tensor_copy(edge_key[1][:, 2:3], dst_side[:, 1:2])
            V.tensor_tensor(cont[:, 0:1], dst_i[:, 0:1], dst_side[:, 0:1], ALU.is_equal)
            V.tensor_tensor(cont[:, 1:COLS], dst_i[:, 1:COLS], dst_i[:, 0:COLS - 1],
                            ALU.is_equal).then_inc(s_const, 1)
            dve.wait_ge(s_keys, 2)

            def onehots(v, b, outs):
                for k, o, n in outs:
                    op = V.tensor_tensor(o[b][:, :, :], col[:, 0:n, :],
                                         keys[:, k, bass.ds(v * UT, UT)].unsqueeze(1).to_broadcast([P, n, UT]),
                                         ALU.is_equal)
                return op

            def count(v, b, i):
                if not at_start(v):
                    dve.wait_ge(a_used, v - 1)
                onehots(v, b, ((0, lo, P), (1, hi, W))).then_inc(a_onehot, 1)

            paired(dve, UNITS, count)

            chain = [0]

            def link(op):
                chain[0] += 1
                op.then_inc(n_chain, 1)
                dve.wait_ge(n_chain, chain[0])

            def prefix(k, counts):
                V.tensor_copy(cnt[k][:, :], counts).then_inc(n_cnt, 1)
                dve.wait_ge(n_cnt, k + 1)
                dve.wait_ge(n_sums, k + 1)
                link(V.tensor_copy(total[:, :], ps_small[1]))
                link(V.tensor_tensor_scan(incl[:, :], ones[:, 0:W], total[:, :], 0.0, ALU.mult, ALU.add))
                link(V.tensor_tensor(incl[:, :], incl[:, :], total[:, :], ALU.subtract))
                link(V.tensor_tensor(base[:, :], incl[:, :], ps_small[0], ALU.add))
                link(V.tensor_scalar(has[:, :], cnt[k][:, :], 0.0, None, ALU.is_gt))
                link(V.tensor_tensor(last[:, :], base[:, :], cnt[k][:, :], ALU.add))
                link(V.scalar_tensor_tensor(last[:, :], last[:, :], float(-1 - E), has[:, :], ALU.add, ALU.mult))
                link(V.tensor_scalar(end_row[k][:, :], last[:, :], float(E), None, ALU.add))

            dve.wait_ge(a_used, UNITS)
            prefix(0, ps_src)
            V.tensor_scalar(base[:, :], base[:, :], 1.0, None, ALU.add).then_inc(n_seed, 1)
            link(V.tensor_scalar(inv_cnt[:, :], cnt[0][:, :], 1.0, None, ALU.max))
            link(V.reciprocal(inv_cnt[:, :], inv_cnt[:, :]))

            def rank_onehots(v, b):
                if not at_start(v):
                    dve.wait_ge(b_picked, v * 2 - 2)
                onehots(v, b, ((0, lo, P), (1, hi, W), (2, dlo, P), (3, dhi, W))).then_inc(b_onehot, 1)

            def place(v, b, h):
                g = v * 2 + h
                dve.wait_ge(b_same, g + 1)
                V.tensor_tensor(same[h][:, :, :], ps_same.rearrange("p (t e) -> p t e", e=P),
                                before_b[:, :].unsqueeze(1).to_broadcast([P, GT, P]),
                                ALU.mult).then_inc(b_masked, 1)
                dve.wait_ge(b_ranked, g + 1)
                V.tensor_tensor(picked[:, :, :], ps_rank[h].rearrange("p (t w) -> p t w", w=W),
                                hi[b % 2][:, :, h * GT:(h + 1) * GT].rearrange("p w t -> p t w"),
                                ALU.mult).then_inc(b_picked, 1)
                dve.wait_ge(b_picked, g + 1)
                dve.wait_ge(b_rows, g + 1)
                V.tensor_reduce(rank[b][h][:, :], picked[:, :, :], AX, ALU.add).then_inc(b_pos, 1)

            def unit(v, b, i):
                if not at_end(v, UNITS):
                    rank_onehots(v + 1, (b + 1) % 2)
                place(v, b, 0)
                if not at_end(v, UNITS):
                    place(v, b, 1)

            dve.wait_ge(s_keys, 4)
            rank_onehots(0, 0)
            rounds(dve, UNITS, DEEP, unit)

            dve.wait_ge(b_ranked, GROUPS)
            prefix(1, ps_dst)
            V.tensor_scalar(last[:, :], cnt[1][:, :], 1.0, None, ALU.add).then_inc(n_deg, 1)
            dve.wait_ge(n_root, 1)
            link(V.reciprocal(dis[:, :], root[:, :]))
            dve.wait_ge(s_xb, 1)
            dve.wait_ge(s_w, WLOAD)
            link(V.scalar_tensor_tensor(bias0[:, :], bcol[:, 1:2], bcol[:, 2:3], bcol[:, 0:1],
                                        ALU.mult, ALU.add))

            def scan(g, h, i):
                dve.wait_ge(c_in[h], i * 32 + 32)
                if not (isinstance(g, int) and g == 0):
                    dve.wait_ge(c_scan, g)
                e = scan_in[h].rearrange("p (j f) -> p j f", f=ROW)
                V.tensor_tensor(flag[:, :], e[:, 1:SJ + 1, A], e[:, 0:SJ, A], ALU.is_equal).then_inc(c_flag, 1)
                dve.wait_ge(c_flag, g * 3 + 1)
                V.tensor_reduce(whole_c[:, bass.ds(g, 1)], flag[:, :], AX, ALU.min)
                V.tensor_scalar(sign[:, :], flag[:, :], 2.0, -1.0, ALU.mult, ALU.add).then_inc(c_flag, 1)
                if isinstance(g, int) and g == 0:
                    V.tensor_copy(first_cont[0][:, :], flag[:, 0:1])
                    V.tensor_copy(edge_key[0][:, 0:1], e[:, 1, A:A + 1])
                if at_end(g, SCHUNKS):
                    V.tensor_copy(edge_key[0][:, 1:2], e[:, SJ, A:A + 1])
                dve.wait_ge(c_flag, g * 3 + 2)
                V.tensor_scalar(limit[:, :], sign[:, :], BIG, None, ALU.mult).then_inc(c_flag, 1)
                dve.wait_ge(c_flag, g * 3 + 3)
                if not at_start(g):
                    dve.wait_ge(c_out[h], i * 16)
                for f in range(A):
                    for at, ctl, op0, op1, none in ((f, flag, ALU.mult, ALU.add, 0.0),
                                                    (A + f, limit, ALU.min, ALU.max, -BIG)):
                        before_it = none if isinstance(g, int) and g == 0 else scan_out[1 - h][:, SJ - 1, at:at + 1]
                        op = V.tensor_tensor_scan(scan_out[h][:, :, at], ctl[:, :], e[:, 1:SJ + 1, f],
                                                  before_it, op0, op1)
                op.then_inc(c_scan, 1)

            paired(dve, SCHUNKS, scan)

            def carries(mode):
                base_k, step = 8 * mode, [0]
                k = min(mode, 1)

                def klink(op):
                    step[0] += 1
                    op.then_inc(k_chain, 1)
                    dve.wait_ge(k_chain, base_k + step[0])

                if mode == 0:
                    dve.wait_ge(c_scan, SCHUNKS)
                    klink(V.tensor_reduce(whole[0][:, :], whole_c[:, :], AX, ALU.min))
                    dve.wait_ge(c_next, 16)
                else:
                    dve.wait_ge(g_chain, mode * LINKS)
                    klink(V.tensor_reduce(whole[1][:, :], cont[:, :], AX, ALU.min))
                klink(V.tensor_copy(whole_w[:, :], whole[k][:, 0:1].to_broadcast([P, D])))
                dve.wait_ge(k_turned, mode + 1)
                klink(V.tensor_copy(turned[:, :], ps_turn[0:D, 0:2 * P]))
                klink(V.tensor_scalar(sign_t[:, :], turned[:, 0:P], 2.0, -1.0, ALU.mult, ALU.add))
                klink(V.tensor_scalar(limit_t[:, :], sign_t[:, :], BIG, None, ALU.mult))
                S = A if mode == 0 else D
                klink(V.tensor_tensor_scan(carry_t[0:S, 1:P + 1], turned[0:S, 0:P], turned[0:S, P:2 * P],
                                           0.0, ALU.mult, ALU.add))
                if mode == 0:
                    klink(V.tensor_tensor_scan(carry_t[A:D, 1:P + 1], limit_t[A:D, :], turned[A:D, P:2 * P],
                                               -BIG, ALU.min, ALU.max))
                else:
                    klink(V.memset(carry_t[:, 0:1], 0.0))
                f0 = first_cont[0][:, :] if mode == 0 else cont[:, 0:1]
                key = edge_key[k]
                if mode < 2:
                    link(V.tensor_tensor(work[:, 0:1], key[:, 1:2], key[:, 2:3], ALU.is_equal))
                    link(V.tensor_tensor(work[:, 1:2], work[:, 0:1], whole[k][:, :], ALU.mult))
                    link(V.tensor_scalar(work[:, 2:3], work[:, 1:2], -1.0, 1.0, ALU.mult, ALU.add))
                    link(V.tensor_tensor(work[:, 0:1], work[:, 2:3], f0, ALU.mult))
                    link(V.scalar_tensor_tensor(work[:, 1:2], key[:, 0:1], float(-NPAD), work[:, 0:1],
                                                ALU.add, ALU.mult))
                    link(V.tensor_scalar(target[k][:, :], work[:, 1:2], float(NPAD), None, ALU.add))
                dve.wait_ge(k_back, mode + 1)
                klink(V.tensor_copy(carry[:, :], ps_turn[:, 2 * P:2 * P + D]))


            def node_stage(mode):
                def window(t, g):
                    return t[:, bass.ds(g * SW, SW), :]

                def wide(t, g, n):
                    return t[:, bass.ds(g * SW, SW)].unsqueeze(2).to_broadcast([P, SW, n])

                def features(g, h, i):
                    step = [0]

                    def mlink(op):
                        step[0] += 1
                        op.then_inc(m_link, 1)
                        dve.wait_ge(m_link, g * 2 + (2 * mode * STEPS + step[0]))

                    for k in range(SW):
                        dve.wait_ge(m_got[h][k], i * 16 + 16 * (mode * STEPS // 2 + 1))
                    dve.wait_ge(m_corr[h], i * 16 + 16 * (mode * STEPS // 2 + 1))
                    c = cat[h]
                    if mode == 0:
                        mlink(V.tensor_tensor(c[:, :, 0:A], window(agg, g)[:, :, 0:A], corr[h][:, :, 0:A], ALU.add))
                        mlink(V.tensor_tensor(c[:, :, A:D], window(agg, g)[:, :, A:D], corr[h][:, :, A:D], ALU.max))
                        V.tensor_tensor(c[:, :, D:3 * A], c[:, :, 0:A], wide(inv_cnt, g, A),
                                        ALU.mult).then_inc(m_cat, 1)
                    else:
                        dve.wait_ge(m_cat, g + mode * STEPS)
                        mlink(V.tensor_tensor(sq[:, :, :], window(agg, g), corr[h][:, :, :], ALU.add))
                        mlink(V.tensor_tensor(sq[:, :, :], sq[:, :, :], window(ys, g), ALU.add))
                        V.tensor_tensor(c[:, :, 0:D], sq[:, :, :], wide(dis, g, D), ALU.mult).then_inc(m_cat, 1)

                def result(g, h, i):
                    if mode == 1:
                        dve.wait_ge(m_node, g + (STEPS + 1))
                        V.tensor_tensor(window(ys, g), ps_node.rearrange("p (t f) -> p t f", f=D),
                                        wide(dis, g, D), ALU.mult).then_inc(m_done, 1)
                        return
                    step = [0]
                    first = 0 if mode == 0 else 7 * STEPS

                    def clink(op):
                        step[0] += 1
                        op.then_inc(m_chain, 1)
                        dve.wait_ge(m_chain, g * 7 + (first + step[0]))

                    def spread(k):
                        return stat[:, k, :].unsqueeze(2).to_broadcast([P, SW, D])

                    if mode == 0:
                        dve.wait_ge(m_node, g + 1)
                        clink(V.tensor_tensor(mid[:, :, :], ps_node.rearrange("p (t f) -> p t f", f=D),
                                              window(xs, g), ALU.add))
                    else:
                        dve.wait_ge(m_cat, g + (2 * STEPS + 2) if not at_end(g, STEPS) else 3 * STEPS)
                        dve.wait_ge(m_done, g + 2 * STEPS)
                        clink(V.tensor_tensor(mid[:, :, :], cat[h][:, :, 0:D], window(xs, g), ALU.add))
                    clink(V.tensor_reduce(stat[:, 0, :], mid[:, :, :], AX, ALU.add))
                    clink(V.tensor_scalar(stat[:, 0, :], stat[:, 0, :], -1.0 / D, None, ALU.mult))
                    clink(V.tensor_tensor(mid[:, :, :], mid[:, :, :], spread(0), ALU.add))
                    clink(V.tensor_tensor(sq[:, :, :], mid[:, :, :], mid[:, :, :], ALU.mult))
                    clink(V.tensor_reduce(stat[:, 0, :], sq[:, :, :], AX, ALU.add))
                    V.tensor_scalar(stat[:, 1, :], stat[:, 0, :], 1.0 / D, EPS, ALU.mult, ALU.add).then_inc(m_var, 1)
                    dve.wait_ge(m_root, g + (mode // 2 * STEPS + 1))
                    clink(V.reciprocal(stat[:, 3, :], stat[:, 2, :]))
                    if mode == 0:
                        V.tensor_tensor(window(xs, g), mid[:, :, :], spread(3), ALU.mult).then_inc(s_xready, 1)
                        dve.wait_ge(s_xready, g + 1)
                        V.tensor_tensor(window(ys, g), window(xs, g), wide(dis, g, D),
                                        ALU.mult).then_inc(m_done, 1)
                    else:
                        if not at_start(g):
                            dve.wait_ge(m_store[h], i * 16 + 16 * STEPS)
                        V.tensor_tensor(res[h][:, :, :], mid[:, :, :], spread(3), ALU.mult).then_inc(m_done, 1)

                features(0, 0, 0)
                features(1, 1, 0)

                def body(g, h, i):
                    result(g, h, i)
                    features(g + 2, h, i + 1)
                paired(dve, STEPS - 2, body)
                result(STEPS - 2, 0, STEPS // 2 - 1)
                result(STEPS - 1, 1, STEPS // 2 - 1)

            carries(0)
            node_stage(0)
            for q in range(2):
                def add_up(g, h, i):
                    if not at_start(g):
                        dve.wait_ge(g_chain, g * CJ + (q * LINKS - CJ - 1))
                    V.tensor_copy(gflag[h][:, :], cont[:, bass.ds(g * CJ, CJ)]).then_inc(g_flag, 1)
                    dve.wait_ge(g_flag, g + (q * CHUNKS + 1))
                    for j in range(CJ):
                        dve.wait_ge(g_got[h][j], i * 16 + (scattered[h * CJ + j] + 16 * q * G_HALF[h] + 16))
                        if isinstance(g, int) and g == 0 and j == 0:
                            continue
                        if not (isinstance(g, int) and g == 0 and j == 1 and q == 0):
                            dve.wait_ge(g_chain, g * CJ + (q * LINKS + j - 1))
                        prior = got_rows[h][:, j - 1, :] if j else got_rows[1 - h][:, CJ - 1, :]
                        V.scalar_tensor_tensor(got_rows[h][:, j, :], prior, gflag[h][:, j:j + 1],
                                               got_rows[h][:, j, :], ALU.mult, ALU.add).then_inc(g_chain, 1)
                if q == 0:
                    dve.wait_ge(m_done, STEPS)
                    V.tensor_tensor(xs[:, :, :], xs[:, :, :], c2_s[:, :].unsqueeze(1).to_broadcast([P, W, D]),
                                    ALU.add)
                paired(dve, CHUNKS, add_up)
                carries(q + 1)
                node_stage(q + 1)


_INS = ["x", "src", "dst", "edge_attr_32", "L0_gnn_u", "L0_gnn_W1", "L0_gnn_b1", "L0_gnn_W2", "L0_gnn_b2",
        "L1_gnn_W1", "L1_gnn_b1", "L1_gnn_W2", "L1_gnn_b2"]


def kernel(**inputs):
    import numpy as np
    import concourse.bacc as bacc
    from concourse.bass_utils import run_bass_kernel_spmd as run

    nc = bacc.Bacc("TRN2", target_bir_lowering=False, num_devices=1)
    arrays, args = {}, []
    for name in _INS:
        a = np.ascontiguousarray(inputs[name])
        arrays[f"in_{name}"] = a
        args.append(nc.dram_tensor(f"in_{name}", a.shape, mybir.dt.from_np(a.dtype), kind="ExternalInput").ap())
    result = nc.dram_tensor("result", (N, D), F32, kind="ExternalOutput").ap()
    build(nc, *args, result)
    r = run(nc, [arrays], core_ids=[0])
    return r.results[0]["result"]
```
